# Optimizing a Trainium2 kernel written in Bass

```python
import numpy as np
import jax
import jax.numpy as jnp

def _softmax(x, axis=-1):
    return jax.nn.softmax(x, axis=axis)

def _gelu(x):
    return jax.nn.gelu(x, approximate=True)

def _silu(x):
    return jax.nn.silu(x)

def _sigmoid(x):
    return jax.nn.sigmoid(x)

def _layernorm(x, axis=-1, eps=1e-05):
    m = jnp.mean(x, axis=axis, keepdims=True)
    v = jnp.var(x, axis=axis, keepdims=True)
    return (x - m) / jnp.sqrt(v + eps)

def _scatter_add(tgt, idx, src, axis=0):
    return tgt.at[idx].add(src)

def _segment_sum(src, seg, n):
    return jax.ops.segment_sum(src, seg, n)
kernel_name = 'mk_prb_d1_jaxref_r8_b3f696'

def setup_inputs(seed: int=0):
    np.random.seed(seed)
    _w = jnp.asarray

    def _L0_attn_setup():
        import jax, jax.numpy as jnp
        import numpy as np
        B, S, DM = (2, 256, 128)
        H, F = (16, 16)
        DH = DM // H
        EPS = 1e-09
        X_NORM = float(np.sqrt(np.sqrt(F)))
        X2_NORM = float(np.sqrt(F))

        def feature_map(x):
            x2 = (x[..., :, None] * x[..., None, :]).reshape(*x.shape[:-1], F * F)
            x2 = x2 / jnp.sqrt(jnp.asarray(2.0, x.dtype))
            ones = jnp.ones_like(x[..., :1])
            return jnp.concatenate([ones, x / X_NORM, x2 / X2_NORM], axis=-1)
        key = jax.random.key(seed)
        k0, k1, k2, k3, k4 = jax.random.split(key, 5)
        hidden_states = jax.random.normal(k0, (B, S, DM), dtype=jnp.float32)
        scale = 1.0 / np.sqrt(DM)
        Wq = jax.random.normal(k1, (DM, H * F), dtype=jnp.float32) * scale
        Wk = jax.random.normal(k2, (DM, H * F), dtype=jnp.float32) * scale
        Wv = jax.random.normal(k3, (DM, H * DH), dtype=jnp.float32) * scale
        Wo = jax.random.normal(k4, (H * DH, DM), dtype=jnp.float32) * scale
        return {'hidden_states': hidden_states, 'Wq': Wq, 'Wk': Wk, 'Wv': Wv, 'Wo': Wo}
    _L0_attn_in = _L0_attn_setup()

    def _L0_ffn_setup():
        import jax, jax.numpy as jnp
        import numpy as np
        H = 128
        I = 64
        E = 8
        K = 2
        SI = I * 2
        B, S = (2, 128)

        def _mlp(x, gw, uw, dw):
            return jax.nn.silu(x @ gw.T) * (x @ uw.T) @ dw.T
        key = jax.random.key(seed)
        ks = jax.random.split(key, 9)
        s = 0.02
        return {'x': jax.random.normal(ks[0], (B, S, H), jnp.float32), 'gate_w': jax.random.normal(ks[1], (E, H), jnp.float32) * s, 'lb_bias': jnp.zeros((E,), jnp.float32), 'expert_gate_w': jax.random.normal(ks[2], (E, I, H), jnp.float32) * s, 'expert_up_w': jax.random.normal(ks[3], (E, I, H), jnp.float32) * s, 'expert_down_w': jax.random.normal(ks[4], (E, H, I), jnp.float32) * s, 'shared_gate_w': jax.random.normal(ks[5], (SI, H), jnp.float32) * s, 'shared_up_w': jax.random.normal(ks[6], (SI, H), jnp.float32) * s, 'shared_down_w': jax.random.normal(ks[7], (H, SI), jnp.float32) * s}
    _L0_ffn_in = _L0_ffn_setup()
    _d = {'L0_attn_hidden_states': _L0_attn_in['hidden_states'], 'L0_attn_Wq': _L0_attn_in['Wq'], 'L0_attn_Wk': _L0_attn_in['Wk'], 'L0_attn_Wv': _L0_attn_in['Wv'], 'L0_attn_Wo': _L0_attn_in['Wo'], 'L0_ffn_gate_w': _L0_ffn_in['gate_w'], 'L0_ffn_lb_bias': _L0_ffn_in['lb_bias'], 'L0_ffn_expert_gate_w': _L0_ffn_in['expert_gate_w'], 'L0_ffn_expert_up_w': _L0_ffn_in['expert_up_w'], 'L0_ffn_expert_down_w': _L0_ffn_in['expert_down_w'], 'L0_ffn_shared_gate_w': _L0_ffn_in['shared_gate_w'], 'L0_ffn_shared_up_w': _L0_ffn_in['shared_up_w'], 'L0_ffn_shared_down_w': _L0_ffn_in['shared_down_w']}
    _x0 = _d['L0_attn_hidden_states']
    _d['L0_attn_hidden_states'] = jax.random.normal(jax.random.fold_in(jax.random.key(seed), 1), (16, 512, 128), dtype=_x0.dtype)
    del _x0
    return _d

def reference(L0_attn_hidden_states, L0_attn_Wq, L0_attn_Wk, L0_attn_Wv, L0_attn_Wo, L0_ffn_gate_w, L0_ffn_lb_bias, L0_ffn_expert_gate_w, L0_ffn_expert_up_w, L0_ffn_expert_down_w, L0_ffn_shared_gate_w, L0_ffn_shared_up_w, L0_ffn_shared_down_w):

    def _L0_attn_ref(hidden_states, Wq, Wk, Wv, Wo):
        import jax, jax.numpy as jnp
        import numpy as np
        B, S, DM = (2, 256, 128)
        H, F = (16, 16)
        DH = DM // H
        EPS = 1e-09
        X_NORM = float(np.sqrt(np.sqrt(F)))
        X2_NORM = float(np.sqrt(F))

        def feature_map(x):
            x2 = (x[..., :, None] * x[..., None, :]).reshape(*x.shape[:-1], F * F)
            x2 = x2 / jnp.sqrt(jnp.asarray(2.0, x.dtype))
            ones = jnp.ones_like(x[..., :1])
            return jnp.concatenate([ones, x / X_NORM, x2 / X2_NORM], axis=-1)
        b, s, _ = hidden_states.shape
        q = (hidden_states @ Wq).reshape(b, s, H, F).transpose(0, 2, 1, 3)
        k = (hidden_states @ Wk).reshape(b, s, H, F).transpose(0, 2, 1, 3)
        v = (hidden_states @ Wv).reshape(b, s, H, DH).transpose(0, 2, 1, 3)
        q = feature_map(q)
        k = feature_map(k)
        qk = jnp.einsum('bhsd,bhtd->bhst', q, k)
        qk = jnp.tril(qk)
        qkv = jnp.einsum('bhst,bhtv->bhsv', qk, v)
        denom = jnp.einsum('bhsd,bhsd->bhs', q, jnp.cumsum(k, axis=2))
        out = qkv / (denom[..., None] + EPS)
        out = out.transpose(0, 2, 1, 3).reshape(b, s, H * DH)
        return out @ Wo

    def _L0_ffn_ref(x, gate_w, lb_bias, expert_gate_w, expert_up_w, expert_down_w, shared_gate_w, shared_up_w, shared_down_w):
        import jax, jax.numpy as jnp
        import numpy as np
        H = 128
        I = 64
        E = 8
        K = 2
        SI = I * 2
        B, S = (2, 128)

        def _mlp(x, gw, uw, dw):
            return jax.nn.silu(x @ gw.T) * (x @ uw.T) @ dw.T
        b, s, h = x.shape
        xf = x.reshape(-1, h)
        logits = xf @ gate_w.T + lb_bias
        scores = jax.nn.sigmoid(logits.astype(jnp.float32))
        topw, topi = jax.lax.top_k(scores, K)
        topw = (topw / (topw.sum(-1, keepdims=True) + 1e-08)).astype(x.dtype)
        out = jnp.zeros_like(xf)
        for e in range(E):
            m = topi == e
            sel = m.any(axis=-1)
            cnt = m.sum()
            wmean = (topw * m).sum() / jnp.maximum(cnt, 1).astype(topw.dtype)
            y = _mlp(xf, expert_gate_w[e], expert_up_w[e], expert_down_w[e])
            out = out + jnp.where(sel[:, None], y * wmean, jnp.zeros((), x.dtype))
        out = out.reshape(b, s, h)
        out = out + _mlp(x, shared_gate_w, shared_up_w, shared_down_w)
        return out
    x = L0_attn_hidden_states
    xn = _layernorm(x, axis=-1)
    x = x + _L0_attn_ref(xn, L0_attn_Wq, L0_attn_Wk, L0_attn_Wv, L0_attn_Wo) + _L0_ffn_ref(xn, L0_ffn_gate_w, L0_ffn_lb_bias, L0_ffn_expert_gate_w, L0_ffn_expert_up_w, L0_ffn_expert_down_w, L0_ffn_shared_gate_w, L0_ffn_shared_up_w, L0_ffn_shared_down_w)
    return x

_drawn_inputs = setup_inputs


def setup_inputs(seed=0):
    import zlib

    import numpy as np

    out = dict(_drawn_inputs(seed))
    spreads = {'L0_ffn_lb_bias': (0.0, 0.8)}
    factors = {'L0_ffn_gate_w': 8.0,
     'L0_ffn_expert_gate_w': 8.0,
     'L0_ffn_expert_up_w': 8.0,
     'L0_ffn_expert_down_w': 8.0,
     'L0_ffn_shared_gate_w': 8.0,
     'L0_ffn_shared_up_w': 8.0,
     'L0_ffn_shared_down_w': 8.0}
    for name, (base, spread) in spreads.items():
        noise = np.random.default_rng([zlib.crc32(name.encode()), seed]).standard_normal(out[name].shape)
        drawn = base * np.exp(spread * noise) if base else spread * noise
        out[name] = jnp.asarray(drawn.astype(out[name].dtype))
    for name, factor in factors.items():
        out[name] = (out[name] * factor).astype(out[name].dtype)
    return out
```

```python
import concourse.bass as bass
from concourse import mybir
from contextlib import ExitStack

NB, S, D = 16, 512, 128
H, F, DV = 16, 16, 8
E, I = 8, 64
P = 128
NC = S // P
NT = NB * NC
GROUP = 4
NG = H // GROUP
UNITS = GROUP + 1
SLOTS = NG * UNITS
OCT = 8
NOCT = H // OCT
TILES = E * I // P + 1
HID = TILES * P
PARTS = 3
Q_SLOTS = (0, 1, 2, 0, 1, 0)
K_SLOTS = (0, 0, 0, 1, 1, 2)
KROWS = F * len(Q_SLOTS)
VW = 32
LN_EPS, TOP_EPS, ATT_EPS = 1e-5, 1e-8, 1e-9
GONE = 1e30
MASKS = 2 * GROUP + 1

GATE, UP, WQ, WK, WV = 0, HID, 2 * HID, 2 * HID + H * F, 2 * HID + 2 * H * F
WCOLS = WV + H * DV


def moe_attention_program(nc, x, w_in, w_v, w_o, w_down, w_route, route_bias, out):
    fp32, bf16, fp32r, i32 = mybir.dt.float32, mybir.dt.bfloat16, mybir.dt.float32r, mybir.dt.int32
    ALU, ACT, AX = mybir.AluOpType, mybir.ActivationFunctionType, mybir.AxisListType
    ctx = ExitStack()
    with ctx:
        def sb(name, shape, dt=fp32):
            return ctx.enter_context(nc.sbuf_tensor(name, shape, dt))

        def sem(name):
            return ctx.enter_context(nc.semaphore(name))

        def scratch(name, shape, dt=fp32):
            return nc.dram_tensor(name, shape, dt, kind="Internal").ap()

        parts_d = [[scratch(f"parts_{n}{o}", [PARTS, F, OCT, S], bf16) for o in range(NOCT)] for n in "qk"]
        sums_d = scratch("sums", [DV + 1, H, S])
        recip_d = scratch("recip", [H, S])

        xnT = sb("xnT", [P, NB * S])
        wts = sb("wts", [P, 2, UNITS, 1024])
        x_all = wts[:].rearrange("p a u n -> p (a u n)")[:, 0:NT * D]
        w_raw = wts[:].rearrange("p a u n -> p (a u n)")[:, NT * D:NT * D + WCOLS]
        q_st = sb("q_stack", [KROWS, NOCT, OCT, S], bf16)
        k_st = sb("k_stack", [KROWS, NOCT, OCT, S], bf16)
        qk_parts = sb("qk_parts", [P, 2 * NOCT, PARTS, S], bf16)
        rest = sb("rest", [P, 2, S])
        w_hi, w_lo = sb("w_hi", [P, WCOLS], fp32r), sb("w_lo", [P, WCOLS], fp32r)
        wv_s, wo_s = sb("wv", [P, H * DV]), sb("wo", [P, D])
        wd_s = sb("wd", [P, TILES, D])
        wr_s, bias_s = sb("wr", [P, E]), sb("route_bias_s", [P, E])
        xa_hi, xa_lo = sb("xa_hi", [P, S], fp32r), sb("xa_lo", [P, S], fp32r)
        xb_hi, xb_lo = sb("xb_hi", [P, S], fp32r), sb("xb_lo", [P, S], fp32r)
        xv = sb("xv", [P, S])
        vp = sb("v_padded", [P, NC, H, VW])
        raw = sb("raw_sums", [P, NG, S])
        num, rec, cum, att = sb("num", [P, S]), sb("rec", [P, S]), sb("cum", [P, S]), sb("att", [P, S])
        den, denr, count = sb("den", [P, S // OCT]), sb("denr", [P, S // OCT]), sb("count", [P, S // OCT])
        count_i = sb("count_i", [P, S // OCT], i32)
        ones = sb("ones", [P, S])
        sil = sb("sil", [P, 2, S])
        hid = sb("hid", [P, TILES, S])
        xres, y = sb("xres", [P, NC, D]), sb("y", [P, NC, D])
        ident, ident_b = sb("ident", [P, P]), sb("ident_b", [P, P], bf16)
        expand = sb("expand", [P, TILES - 1, 2, I], bf16)
        unsel = sb("unsel", [P, NT, E])
        unsel_p = sb("unsel_p", [P, NC, P], bf16)
        unselT = sb("unselT", [P, S], bf16)
        logit = sb("logit", [P, NT, E])
        stat = sb("stat", [P, NT, 6])
        mean, var, rstd, tmp = (sb(n, [P, NT]) for n in ("mean", "var", "rstd", "tmp"))
        m1, m2, t1, sw = (sb(n, [P, NT]) for n in ("m1", "m2", "t1", "sw"))
        order = sb("order", [P, E])
        per_e, wmean = sb("per_e", [P, 2, E]), sb("wmean", [P, 2, E])
        score, one1, one2, rt = (hid[:, n, :].rearrange("p (c e) -> p c e", e=E) for n in range(4))
        xn = num[:].rearrange("p (c d) -> p c d", d=D), cum[:].rearrange("p (c d) -> p c d", d=D)

        x_stage = xv, att
        ps_s = ctx.enter_context(nc.psum_tensor("ps_s", [P, 2, 1024], fp32))
        ps_av = ctx.enter_context(nc.psum_tensor("ps_av", [P, S], fp32))
        ps_x = [ctx.enter_context(nc.psum_tensor(f"ps_x{n}", [P, S], fp32)) for n in range(3)]
        logit_bank = ps_x[2], ps_av
        (B_SEL, B_VT, B_G0, B_U0, B_G1, B_V, B_U1, B_G2, B_U2, B_G3, B_U3, B_G4, B_U4,
         B_Q0, B_K0, B_Q1, B_K1, B_OUT) = (ps_x[n % 3] for n in range(18))
        B_G, B_U, B_P = (B_G0, B_G1, B_G2, B_G3, B_G4), (B_U0, B_U1, B_U2, B_U3, B_U4), (B_Q0, B_K0, B_Q1, B_K1)

        x_in, w_in_sem, xt_ready, xn_ready, stats_step, rstd_step = (sem(n) for n in (
            "x_in", "w_in_sem", "xt_ready", "xn_ready", "stats_step", "rstd_step"))
        biased = sem("biased")
        var_ready, sqrt_ready, xnT_ready, logits_ps, logits_ready = (sem(n) for n in (
            "var_ready", "sqrt_ready", "xnT_ready", "logits_ps", "logits_ready"))
        scores_e, route_step, per_e_ready, wmean_ps, wd_ready = (sem(n) for n in (
            "scores_e", "route_step", "per_e_ready", "wmean_ps", "wd_ready"))
        consts, const_step, w_split, w_split_hi, unsel_ready = (sem(n) for n in (
            "consts", "const_step", "w_split", "w_split_hi", "unsel_ready"))
        turns = sem("turns")
        scores_ready = sem("scores_ready")
        squares_ready = sem("squares_ready")
        masked = sem("masked")
        av_ready = sem("av_ready")
        raw_ready = sem("raw_ready")
        selT_ps, selT_ready, unsel_p_ready = sem("selT_ps"), sem("selT_ready"), sem("unsel_p_ready")
        vt_ps, cum_ready = sem("vt_ps"), sem("cum_ready")
        gate_ps, up_ps, silu_ready, hid_ready = sem("gate_ps"), sem("up_ps"), sem("silu_ready"), sem("hid_ready")
        v_ps, vp_ready = sem("v_ps"), sem("vp_ready")
        qk_ps, part0_ready, rest_ready, part1_ready, part2_ready = (sem(n) for n in (
            "qk_ps", "part0_ready", "rest_ready", "part1_ready", "part2_ready"))
        xb_hi_ready, xb_ready, xa_hi_ready, xa_ready, xv_ready = (sem(n) for n in (
            "xb_hi_ready", "xb_ready", "xa_hi_ready", "xa_ready", "xv_ready"))
        den_sum, recip_ready, num_sum, att_ready, out_ps, y_ready = (sem(n) for n in (
            "den_sum", "recip_ready", "num_sum", "att_ready", "out_ps", "y_ready"))
        parts_out = [sem(f"parts_out{o}") for o in range(NOCT)]
        stack_in = [sem(f"stack_in{o}") for o in range(NOCT)]
        STACK_DMAS = 9
        xres_in, sums_out, num_in, den_in, recip_out, rec_in, y_out = (sem(n) for n in (
            "xres_in", "sums_out", "num_in", "den_in", "recip_out", "rec_in", "y_out"))

        block = ctx.enter_context(nc.Block())

        def batch_cols(b):
            return bass.ds(b * S, S) if not isinstance(b, int) else slice(b * S, b * S + S)

        def rows_of(t, b):
            return t[bass.ds(b, 1)].rearrange("a (c p) d -> p (a c) d", p=P)

        @block.sync
        def _(sp):
            for n in range(4):
                q = NB // 4
                sp.dma_start(x_all[:, n * q * NC * D:(n + 1) * q * NC * D].rearrange("p (k d) -> p k d", d=D),
                             x[n * q:(n + 1) * q].rearrange("b (c p) d -> p (b c) d", p=P)).then_inc(x_in, 16)
                sp.wait_ge(x_in, 16 * (n + 1))
            for dst, src in ((w_raw, w_in), (wv_s[:], w_v), (wo_s[:], w_o), (wd_s[:], w_down), (wr_s[:], w_route),
                             (bias_s[:], route_bias.partition_broadcast(P))):
                sp.dma_start(dst, src).then_inc(w_in_sem, 16)

            def parts_to_dram(b, o):
                sp.wait_ge(part2_ready, b * 4 + 2 * o + 2)
                sp.sem_inc(turns, 1)
                if not isinstance(b, int) or b > 0:
                    sp.wait_ge(stack_in[o], b * (16 * STACK_DMAS))
                for n in range(2):
                    sp.dma_start(parts_d[n][o].rearrange("r f h s -> (f h) r s"),
                                 qk_parts[:, 2 * o + n]).then_inc(parts_out[o], 16)

            def stacks_from_dram(b, o):
                sp.wait_ge(parts_out[o], b * 32 + 32)
                if not isinstance(b, int) or b > 0:
                    sp.wait_ge(scores_ready, (b - 1) * SLOTS + 2 * UNITS * (o + 1))
                q_rows = parts_d[0][o].rearrange("r f h s -> (r f) (h s)")
                k_rows = parts_d[1][o].rearrange("r f h s -> (r f) (h s)")
                row = 0
                for n in (3, 2, 1):
                    sp.dma_start(q_st[row:row + n * F, o].rearrange("p h s -> p (h s)"),
                                 q_rows[0:n * F]).then_inc(stack_in[o], 16)
                    row += n * F
                for r, part in enumerate(K_SLOTS):
                    sp.dma_start(k_st[r * F:(r + 1) * F, o].rearrange("p h s -> p (h s)"),
                                 k_rows[part * F:(part + 1) * F]).then_inc(stack_in[o], 16)

            def iteration(i, attend, experts, project):
                f, n = i - 1, i + 1
                if attend:
                    stacks_from_dram(i, 1)
                if experts:
                    if not isinstance(f, int) or f > 0:
                        sp.wait_ge(y_ready, f)
                        sp.sem_inc(turns, 1)
                    sp.dma_start(xres[:], rows_of(x, f)).then_inc(xres_in, 16)
                    sp.wait_ge(raw_ready, f * NG + NG)
                    for j in range(GROUP):
                        sp.dma_start(sums_d[:, j * NG:(j + 1) * NG, :],
                                     raw[32 * j:32 * j + DV + 1]).then_inc(sums_out, 16)
                    sp.wait_ge(sums_out, f * (16 * GROUP) + 16 * GROUP)
                    sp.dma_start(den[:], sums_d[DV].rearrange("h (k s) -> (h k) s", s=S // OCT)).then_inc(den_in, 16)
                    if not isinstance(f, int) or f > 0:
                        sp.wait_ge(num_sum, f)
                    sp.dma_start(num[:], sums_d[0:DV].rearrange("d h s -> (d h) s")).then_inc(num_in, 16)
                    sp.wait_ge(recip_ready, f + 1)
                    sp.dma_start(recip_d.rearrange("h (k s) -> (h k) s", s=S // OCT), denr[:]).then_inc(recip_out, 16)
                    sp.wait_ge(recip_out, f * 16 + 16)
                    if not isinstance(f, int) or f > 0:
                        sp.wait_ge(att_ready, f)
                    for d in range(DV):
                        sp.dma_start(rec[d * H:(d + 1) * H, :], recip_d).then_inc(rec_in, 16)
                if project:
                    parts_to_dram(n, 0)
                    stacks_from_dram(n, 0)
                    parts_to_dram(n, 1)
                if experts:
                    sp.wait_ge(y_ready, f + 1)
                    sp.sem_inc(turns, 1)
                    sp.dma_start(rows_of(out, f), y[:]).then_inc(y_out, 16)

            parts_to_dram(0, 0)
            stacks_from_dram(0, 0)
            parts_to_dram(0, 1)
            iteration(0, True, False, True)
            with sp.Fori(1, NB - 1) as i:
                iteration(i, True, True, True)
            iteration(NB - 1, True, True, False)
            iteration(NB, False, True, False)
            sp.wait_ge(y_out, 16 * NB)

        @block.gpsimd
        def _(pool):
            nc.gpsimd.memset(ident[:], 0.0).then_inc(const_step, 1)
            nc.gpsimd.memset(ident_b[:], 0.0).then_inc(const_step, 1)
            nc.gpsimd.memset(expand[:], GONE).then_inc(const_step, 1)
            nc.gpsimd.memset(vp[:], 0.0).then_inc(const_step, 1)
            nc.gpsimd.memset(unsel_p[:], 0.0).then_inc(const_step, 1)
            nc.gpsimd.memset(ones[:], 1.0).then_inc(const_step, 1)
            pool.wait_ge(const_step, 6)
            for m in (ident, ident_b):
                nc.gpsimd.affine_select(out=m[:], in_=m[:], compare_op=ALU.not_equal, fill=1.0, base=0,
                                        pattern=[[-1, P]], channel_multiplier=1).then_inc(consts, 1)
            nc.gpsimd.affine_select(out=expand[:], in_=expand[:], compare_op=ALU.is_equal, fill=0.0, base=0,
                                    pattern=[[-2, TILES - 1], [-1, 2], [0, I]], channel_multiplier=1).then_inc(consts, 1)
            nc.gpsimd.memset(vp[:, :, :, DV:DV + 1], 1.0).then_inc(consts, 1)
            nc.gpsimd.iota(order[:], pattern=[[-1, E]], base=E, channel_multiplier=0,
                           allow_small_or_imprecise_dtypes=True).then_inc(consts, 1)
            nc.gpsimd.iota(count_i[:], pattern=[[1, S // OCT]], base=0, channel_multiplier=S // OCT).then_inc(consts, 1)

            def mask(b, u):
                g, j = divmod(u, UNITS)
                w = wts[:, g % 2, j, :]
                pool.wait_ge(squares_ready, b * SLOTS + u + 1)
                pool.sem_inc(turns, 1)
                keep = dict(compare_op=ALU.is_ge, fill=0.0, base=0, channel_multiplier=-1)
                if j < GROUP:
                    v = w.rearrange("p (a n) -> p a n", a=2)[:, :, 0:P]
                    nc.gpsimd.affine_select(out=v, in_=v, pattern=[[0, 2], [1, P]], **keep).then_inc(masked, 1)
                    v = w[:, 1024 - P:1024]
                    nc.gpsimd.affine_select(out=v, in_=v, pattern=[[1, P]], **keep).then_inc(masked, 1)
                else:
                    v = w.rearrange("p (a n) -> p a n", a=GROUP)[:, :, 0:P]
                    nc.gpsimd.affine_select(out=v, in_=v, pattern=[[0, GROUP], [1, P]], **keep).then_inc(masked, 1)

            def iteration(i, attend, experts):
                f = i - 1
                if experts:
                    if not isinstance(f, int):
                        pool.wait_ge(selT_ps, f)
                    elif f == 0:
                        pool.wait_ge(unsel_ready, 1)
                    else:
                        pool.wait_ge(selT_ps, f)
                    chunks = bass.ds(f * NC, NC) if not isinstance(f, int) else slice(f * NC, f * NC + NC)
                    nc.gpsimd.tensor_copy(unsel_p[:, :, 0:E], unsel[:, chunks, :]).then_inc(unsel_p_ready, 1)
                if attend:
                    for u in range(SLOTS):
                        mask(i, u)

            iteration(0, True, False)
            pool.wait_ge(unsel_ready, 1)
            with pool.Fori(1, NB) as i:
                iteration(i, True, True)
            iteration(NB, False, True)

        @block.scalar
        def _(act):
            act.wait_ge(var_ready, 1)
            nc.scalar.activation(tmp[:], var[:], ACT.Sqrt).then_inc(sqrt_ready, 1)
            with act.Fori(0, NB // 2) as k:
                for par in range(2):
                    b = k * 2 + par
                    act.wait_ge(xt_ready, b + 1)
                    nc.scalar.activation(xnT[:, batch_cols(b)], ps_x[par][:], ACT.Copy).then_inc(xnT_ready, 1)
                    nc.scalar.activation(x_stage[par][:], ps_x[par][:], ACT.Copy).then_inc(xnT_ready, 1)
                for par in range(2):
                    b = k * 2 + par
                    act.wait_ge(logits_ps, b + 1)
                    nc.scalar.activation(logit[:, bass.ds(b * NC, NC), :], logit_bank[par][:, 0:NC * E].rearrange(
                        "p (c e) -> p c e", e=E), ACT.Copy).then_inc(logits_ready, 1)
            act.wait_ge(biased, 1)
            nc.scalar.activation(score, logit[:], ACT.Sigmoid).then_inc(scores_e, 1)

            def square(b, u):
                g, j = divmod(u, UNITS)
                act.wait_ge(scores_ready, b * SLOTS + u + 1)
                if j == 0 and not (isinstance(b, int) and b == 0 and g < 2):
                    act.wait_ge(av_ready, b * NG + g - 1)
                nc.scalar.activation(wts[:, g % 2, j, :], ps_s[:, u % 2, :], ACT.Square, bias=1.0,
                                     scale=0.25).then_inc(squares_ready, 1)

            def sums_out_of_psum(b, g):
                act.wait_ge(av_ready, b * NG + g + 1)
                if g == 0 and not (isinstance(b, int) and b == 0):
                    act.wait_ge(sums_out, b * (16 * GROUP))
                nc.scalar.activation(raw[:, g, :], ps_av[:], ACT.Copy).then_inc(raw_ready, 1)

            def silu(b, j):
                act.wait_ge(gate_ps, b * TILES + j + 1)
                if j >= 2:
                    act.wait_ge(hid_ready, b * TILES + j - 1)
                elif not (isinstance(b, int) and b == 0):
                    act.wait_ge(hid_ready, b * TILES)
                nc.scalar.activation(sil[:, j % 2, :], B_G[j][:], ACT.Silu).then_inc(silu_ready, 1)

            def part0(b, t):
                act.wait_ge(qk_ps, b * 4 + t + 1)
                if not (isinstance(b, int) and b == 0):
                    act.wait_ge(parts_out[t // 2], b * 32)
                nc.scalar.activation(qk_parts[:, t, 0, :], B_P[t][:], ACT.Copy).then_inc(part0_ready, 1)

            def v_out(b):
                act.wait_ge(v_ps, b + 1)
                if not (isinstance(b, int) and b == 0):
                    act.wait_ge(av_ready, b * NG)
                else:
                    act.wait_ge(consts, 6)
                nc.scalar.activation(vp[:].rearrange("p c h w -> p (c h) w")[:, :, 0:DV],
                                     B_V[:].rearrange("p (k d) -> p k d", d=DV), ACT.Copy).then_inc(vp_ready, 1)

            def iteration(i, attend, experts, project):
                f, n = i - 1, i + 1
                for u in range(SLOTS):
                    if attend:
                        square(i, u)
                    if u == 0 and experts:
                        act.wait_ge(selT_ps, f + 1)
                        nc.scalar.activation(unselT[:], B_SEL[:], ACT.Copy).then_inc(selT_ready, 1)
                    if experts and u in (1, 3, 5, 7, 9):
                        silu(f, (u - 1) // 2)
                    if u == 4:
                        if experts:
                            sums_out_of_psum(f, NG - 1)
                        if attend:
                            v_out(i)
                    if attend and u in (9, 14, 19):
                        sums_out_of_psum(i, u // UNITS - 1)
                    if project and 11 <= u <= 14:
                        part0(n, u - 11)

            for t in range(4):
                part0(0, t)
            iteration(0, True, False, True)
            with act.Fori(1, NB - 1) as i:
                iteration(i, True, True, True)
            iteration(NB - 1, True, True, False)
            iteration(NB, False, True, False)

        @block.vector
        def _(dve):
            steps = {}

            def step(ins, s):
                steps[s.name] = steps.get(s.name, 0) + 1
                ins.then_inc(s, 1)
                dve.wait_ge(s, steps[s.name])

            for n in range(4):
                dve.wait_ge(x_in, 16 * (n + 1))
                with dve.Fori(n * (NT // 4), (n + 1) * (NT // 4)) as c:
                    nc.vector.bn_stats(stat[:, bass.ds(c, 1), :].rearrange("p a n -> p (a n)"),
                                       x_all[:, bass.ds(c * D, D)]).then_inc(stats_step, 1)
            dve.wait_ge(stats_step, NT)
            step(nc.vector.tensor_tensor(mean[:], stat[:, :, 1], stat[:, :, 4], ALU.add), rstd_step)
            step(nc.vector.tensor_scalar(mean[:], mean[:], 0.5, None, ALU.mult), rstd_step)
            step(nc.vector.tensor_tensor(m1[:], stat[:, :, 1], stat[:, :, 4], ALU.subtract), rstd_step)
            step(nc.vector.scalar_tensor_tensor(m1[:], m1[:], 0.25, m1[:], ALU.mult, ALU.mult), rstd_step)
            step(nc.vector.tensor_tensor(m2[:], stat[:, :, 2], stat[:, :, 5], ALU.add), rstd_step)
            step(nc.vector.scalar_tensor_tensor(var[:], m2[:], 1.0 / D, m1[:], ALU.mult, ALU.add), rstd_step)
            nc.vector.tensor_scalar(var[:], var[:], LN_EPS, None, ALU.add).then_inc(var_ready, 1)
            dve.wait_ge(sqrt_ready, 1)
            step(nc.vector.reciprocal(rstd[:], tmp[:]), rstd_step)
            step(nc.vector.tensor_tensor(t1[:], rstd[:], rstd[:], ALU.mult), rstd_step)
            step(nc.vector.scalar_tensor_tensor(t1[:], t1[:], -0.5, var[:], ALU.mult, ALU.mult), rstd_step)
            step(nc.vector.scalar_tensor_tensor(rstd[:], t1[:], 1.5, rstd[:], ALU.add, ALU.mult), rstd_step)
            with dve.Fori(0, NB // 2) as k:
                for par in range(2):
                    b = k * 2 + par
                    if par == 0:
                        dve.wait_ge(xt_ready, k * 2)
                    for c in range(NC):
                        row = b * NC + c
                        nc.vector.tensor_scalar(xn[par][:, c, :], x_all[:, bass.ds(row * D, D)],
                                                mean[:, bass.ds(row, 1)], rstd[:, bass.ds(row, 1)],
                                                ALU.subtract, ALU.mult).then_inc(xn_ready, 1)
            dve.wait_ge(w_in_sem, 16 * 6)
            nc.vector.tensor_copy(w_hi[:], w_raw).then_inc(w_split_hi, 1)
            dve.wait_ge(w_split_hi, 1)
            nc.vector.tensor_tensor(w_lo[:], w_raw, w_hi[:].bitcast(fp32), ALU.subtract).then_inc(w_split, 1)

            def split_x(b, hi, lo, hi_sem, lo_sem):
                nc.vector.tensor_scalar(hi[:], xnT[:, batch_cols(b)], 1.0, None, ALU.mult).then_inc(hi_sem, 1)
                dve.wait_ge(hi_sem, b + 1)
                nc.vector.tensor_tensor(lo[:], xnT[:, batch_cols(b)], hi[:].bitcast(fp32),
                                        ALU.subtract).then_inc(lo_sem, 1)

            def split_tile(b, t):
                r = rest[:, t % 2, :]
                dve.wait_ge(part0_ready, b * 4 + t + 1)
                if t >= 2:
                    dve.wait_ge(part2_ready, b * 4 + t - 1)
                elif not (isinstance(b, int) and b == 0):
                    dve.wait_ge(part2_ready, b * 4 + t - 1)
                nc.vector.tensor_tensor(r, B_P[t][:], qk_parts[:, t, 0, :], ALU.subtract).then_inc(rest_ready, 1)
                dve.wait_ge(rest_ready, b * 4 + t + 1)
                nc.vector.tensor_copy(qk_parts[:, t, 1, :], r).then_inc(part1_ready, 1)
                dve.wait_ge(part1_ready, b * 4 + t + 1)
                nc.vector.tensor_tensor(qk_parts[:, t, 2, :], r, qk_parts[:, t, 1, :],
                                        ALU.subtract).then_inc(part2_ready, 1)

            def hidden(b, j):
                dve.wait_ge(up_ps, b * TILES + j + 1)
                dve.wait_ge(silu_ready, b * TILES + j + 1)
                if j == 0 and not (isinstance(b, int) and b == 0):
                    dve.wait_ge(out_ps, b)
                nc.vector.tensor_tensor(hid[:, j, :], B_U[j][:], sil[:, j % 2, :], ALU.mult).then_inc(hid_ready, 1)

            def copy_xv(b):
                if isinstance(b, int) and b == 0:
                    dve.wait_ge(logits_ps, NB)
                else:
                    dve.wait_ge(v_ps, b)
                nc.vector.tensor_scalar(xv[:], xnT[:, batch_cols(b)], 1.0, None, ALU.mult).then_inc(xv_ready, 1)

            def routing():
                dve.wait_ge(scores_e, 1)
                dve.wait_ge(consts, 6)
                wide = [P, NT, E]
                o = order[:].unsqueeze(1).to_broadcast(wide)

                def b3(t):
                    return t[:].unsqueeze(2).to_broadcast(wide)

                def best(src, m, one):
                    step(nc.vector.tensor_reduce(m[:], src, AX.X, ALU.max), route_step)
                    step(nc.vector.tensor_tensor(rt, src, b3(m), ALU.is_equal), route_step)
                    step(nc.vector.tensor_tensor(rt, rt, o, ALU.mult), route_step)
                    step(nc.vector.tensor_reduce(t1[:], rt, AX.X, ALU.max), route_step)
                    step(nc.vector.tensor_tensor(one, rt, b3(t1), ALU.is_equal), route_step)

                best(score, m1, one1)
                step(nc.vector.scalar_tensor_tensor(score, one1, -4.0, score, ALU.mult, ALU.add), route_step)
                best(score, m2, one2)
                step(nc.vector.tensor_tensor(rt, one1, one2, ALU.add), route_step)
                nc.vector.tensor_scalar(unsel[:], rt, -1.0, None, ALU.add).then_inc(unsel_ready, 1)
                step(nc.vector.tensor_reduce(per_e[:, 1, :], rt.rearrange("p c e -> p e c"), AX.X, ALU.add), route_step)
                step(nc.vector.scalar_tensor_tensor(sw[:], m1[:], TOP_EPS, m2[:], ALU.add, ALU.add), route_step)
                step(nc.vector.reciprocal(sw[:], sw[:]), route_step)
                step(nc.vector.tensor_tensor(m1[:], m1[:], sw[:], ALU.mult), route_step)
                step(nc.vector.tensor_tensor(m2[:], m2[:], sw[:], ALU.mult), route_step)
                step(nc.vector.tensor_tensor(one1, one1, b3(m1), ALU.mult), route_step)
                step(nc.vector.tensor_tensor(one2, one2, b3(m2), ALU.mult), route_step)
                step(nc.vector.tensor_tensor(rt, one1, one2, ALU.add), route_step)
                nc.vector.tensor_reduce(per_e[:, 0, :], rt.rearrange("p c e -> p e c"), AX.X, ALU.add).then_inc(per_e_ready, 1)

            def mean_weights():
                dve.wait_ge(wmean_ps, 1)
                step(nc.vector.tensor_copy(wmean[:], ps_x[2][:, 0:2 * E].rearrange("p (a e) -> p a e", a=2)), route_step)
                step(nc.vector.tensor_scalar(wmean[:, 1, :], wmean[:, 1, :], 1.0, None, ALU.max), route_step)
                step(nc.vector.reciprocal(wmean[:, 1, :], wmean[:, 1, :]), route_step)
                step(nc.vector.tensor_tensor(wmean[:, 0, :], wmean[:, 0, :], wmean[:, 1, :], ALU.mult), route_step)
                dve.wait_ge(w_in_sem, 16 * 6)
                for e in range(E):
                    r = slice(I * (e % 2), I * (e % 2) + I)
                    nc.vector.tensor_scalar(wd_s[r, e // 2, :], wd_s[r, e // 2, :], wmean[r, 0, e:e + 1], None,
                                            ALU.mult).then_inc(wd_ready, 1)
                step(nc.vector.tensor_single_scalar(count_i[:], count_i[:], S - 1, ALU.bitwise_and), route_step)
                step(nc.vector.tensor_copy(count[:], count_i[:]), route_step)
                step(nc.vector.tensor_scalar(count[:], count[:], 1.0, None, ALU.add), route_step)

            def iteration(i, attend, experts, project):
                f, n = i - 1, i + 1
                if project:
                    dve.wait_ge(qk_ps, n * 4)
                    split_x(n, xb_hi, xb_lo, xb_hi_ready, xb_ready)
                if experts:
                    dve.wait_ge(vt_ps, f + 1)
                    nc.vector.tensor_tensor_scan(cum[:], ones[:], B_VT[:], 0.0, ALU.mult, ALU.add).then_inc(cum_ready, 1)
                    for j in range(4):
                        hidden(f, j)
                    dve.wait_ge(den_in, f * 16 + 16)
                    if not isinstance(f, int) or f > 0:
                        dve.wait_ge(recip_out, f * 16)
                    nc.vector.scalar_tensor_tensor(den[:], den[:], 2 * ATT_EPS, count[:], ALU.add,
                                                   ALU.add).then_inc(den_sum, 1)
                    dve.wait_ge(den_sum, f + 1)
                    nc.vector.reciprocal(denr[:], den[:]).then_inc(recip_ready, 1)
                    hidden(f, 4)
                if not experts:
                    routing()
                if attend:
                    if experts:
                        dve.wait_ge(up_ps, f * TILES + TILES)
                    split_x(i, xa_hi, xa_lo, xa_hi_ready, xa_ready)
                if project:
                    split_tile(n, 0)
                    split_tile(n, 1)
                if experts:
                    dve.wait_ge(num_in, f * 16 + 16)
                    dve.wait_ge(cum_ready, f + 1)
                    nc.vector.tensor_tensor(cum[:], num[:], cum[:], ALU.add).then_inc(num_sum, 1)
                    dve.wait_ge(num_sum, f + 1)
                    dve.wait_ge(rec_in, f * (16 * DV) + 16 * DV)
                    if not isinstance(f, int) or f > 0:
                        dve.wait_ge(out_ps, f)
                    nc.vector.tensor_tensor(att[:], cum[:], rec[:], ALU.mult).then_inc(att_ready, 1)
                if project:
                    split_tile(n, 2)
                    split_tile(n, 3)
                    copy_xv(n)
                if not experts:
                    mean_weights()
                if experts:
                    dve.wait_ge(out_ps, f + 1)
                    dve.wait_ge(xres_in, f * 16 + 16)
                    if not isinstance(f, int) or f > 0:
                        dve.wait_ge(y_out, f * 16)
                    nc.vector.tensor_tensor(y[:], B_OUT[:].rearrange("p (c d) -> p c d", d=D), xres[:],
                                            ALU.add).then_inc(y_ready, 1)

            dve.wait_ge(logits_ready, NB)
            nc.vector.tensor_tensor(logit[:], logit[:], bias_s[:].unsqueeze(1).to_broadcast([P, NT, E]),
                                    ALU.add).then_inc(biased, 1)
            dve.wait_ge(xnT_ready, 2 * NB)
            split_x(0, xb_hi, xb_lo, xb_hi_ready, xb_ready)
            for t in range(4):
                split_tile(0, t)
            copy_xv(0)
            iteration(0, True, False, True)
            with dve.Fori(1, NB - 1) as i:
                iteration(i, True, True, True)
            iteration(NB - 1, True, True, False)
            iteration(NB, False, True, False)

        @block.tensor
        def _(pe):
            pe.wait_ge(consts, 6)
            pe.wait_ge(w_in_sem, 16 * 6)
            with pe.Fori(0, NB // 2) as k:
                for par in range(2):
                    b = k * 2 + par
                    pe.wait_ge(xn_ready, b * NC + NC)
                    for c in range(NC):
                        last = nc.tensor.transpose(ps_x[par][:, c * P:(c + 1) * P], xn[par][:, c, :], ident[:])
                    last.then_inc(xt_ready, 1)
                for par in range(2):
                    b = k * 2 + par
                    pe.wait_ge(xnT_ready, b * 2 + 2)
                    pe.wait_ge(logits_ready, k * 2)
                    for c in range(NC):
                        last = nc.tensor.matmul(logit_bank[par][:, c * E:(c + 1) * E],
                                                x_stage[par][:, c * P:(c + 1) * P], wr_s[:], start=True, stop=True)
                    last.then_inc(logits_ps, 1)
            pe.wait_ge(w_split, 1)

            def three(bank, col, hi, lo, stop=True):
                nc.tensor.matmul(bank[:], w_hi[:, col:col + P], hi[:], start=True, stop=False)
                nc.tensor.matmul(bank[:], w_lo[:, col:col + P], hi[:], start=False, stop=False)
                return nc.tensor.matmul(bank[:], w_hi[:, col:col + P], lo[:], start=False, stop=stop)

            def project_tile(b, t):
                o, n = divmod(t, 2)
                col = (WQ, WK)[n] + o * P
                three(B_P[t], col, xb_hi, xb_lo).then_inc(qk_ps, 1)

            def scores(b, u):
                g, j = divmod(u, UNITS)
                o = g // 2
                if not (isinstance(b, int) and b == 0 and u < 2):
                    pe.wait_ge(squares_ready, b * SLOTS + u - 1)
                if u % (2 * UNITS) == 0:
                    pe.wait_ge(stack_in[o], b * (16 * STACK_DMAS) + 16 * STACK_DMAS)

                def chunk(head, key, dst):
                    h = head % OCT
                    return nc.tensor.matmul(dst, k_st[:, o, h, key * P:(key + 1) * P],
                                            q_st[:, o, h, key * P:S], start=True, stop=True)
                ps = ps_s[:, u % 2, :]
                if j < GROUP:
                    chunk(g * GROUP + j, 0, ps[:, 0:512])
                    chunk(g * GROUP + j, 1, ps[:, 512:896])
                    last = chunk(g * GROUP + j, 3, ps[:, 896:1024])
                else:
                    for jj in range(GROUP):
                        last = chunk(g * GROUP + jj, 2, ps[:, jj * 256:(jj + 1) * 256])
                last.then_inc(scores_ready, 1)

            AV = ((0, 0, 512), (1, 512, 896), (3, 896, 1024), (2, None, None))

            def weighted(b, g, n):
                key, lo, hi = AV[n]
                if n == 0:
                    pe.wait_ge(masked, b * (NG * MASKS) + (g + 1) * MASKS)
                    if not (isinstance(b, int) and b == 0 and g == 0):
                        pe.wait_ge(raw_ready, b * NG + g)
                    if g == 0:
                        pe.wait_ge(vp_ready, b + 1)
                for j in range(GROUP):
                    w = wts[:, g % 2, j, lo:hi] if key != 2 else wts[:, g % 2, GROUP, j * 256:(j + 1) * 256]
                    last = nc.tensor.matmul(ps_av[32 * j:32 * j + VW, key * P:S], vp[:, key, g * GROUP + j, :], w,
                                            start=(n == 0), stop=(n == 3))
                if n == 3:
                    last.then_inc(av_ready, 1)

            def gate(b, j):
                last = three(B_G[j], GATE + j * P, xa_hi, xa_lo, stop=(j == TILES - 1))
                if j < TILES - 1:
                    if j == 0:
                        pe.wait_ge(selT_ready, b + 1)
                    last = nc.tensor.matmul(B_G[j][:], expand[:, j].rearrange("p a i -> p (a i)"), unselT[:],
                                            start=False, stop=True)
                last.then_inc(gate_ps, 1)

            def up(b, j):
                three(B_U[j], UP + j * P, xa_hi, xa_lo).then_inc(up_ps, 1)

            def out_chunk(b, c):
                tok = slice(c * P, (c + 1) * P)
                for j in range(TILES):
                    nc.tensor.matmul(B_OUT[:, tok], hid[:, j, tok], wd_s[:, j, :], start=(j == 0), stop=False)
                last = nc.tensor.matmul(B_OUT[:, tok], att[:, tok], wo_s[:], start=False, stop=True)
                if c == NC - 1:
                    last.then_inc(out_ps, 1)

            def iteration(i, attend, experts, project):
                f, n = i - 1, i + 1
                first = isinstance(i, int) and i == 0
                final = isinstance(i, int) and i == NB
                for u in range(SLOTS):
                    g, j = divmod(u, UNITS)
                    if attend:
                        scores(i, u)
                    if j > 0:
                        if g == 0 and experts:
                            weighted(f, NG - 1, j - 1)
                        elif g > 0 and attend:
                            weighted(i, g - 1, j - 1)
                    if experts:
                        if u == 0:
                            pe.wait_ge(unsel_p_ready, f + 1)
                            if final:
                                pe.wait_ge(hid_ready, f * TILES)
                            else:
                                pe.wait_ge(rest_ready, i * 4 + 3)
                            for c in range(NC):
                                last = nc.tensor.matmul(B_SEL[:, c * P:(c + 1) * P], unsel_p[:, c, :], ident_b[:],
                                                        start=True, stop=True)
                            last.then_inc(selT_ps, 1)
                            pe.wait_ge(xa_ready, f + 1)
                            if not final:
                                pe.wait_ge(rest_ready, i * 4 + 4)
                            three(B_VT, WV, xa_hi, xa_lo).then_inc(vt_ps, 1)
                        if u == 1:
                            pe.wait_ge(y_ready, f)
                            pe.wait_ge(wd_ready, E)
                            gate(f, 0)
                        if u == 2:
                            pe.wait_ge(selT_ready, f + 1)
                            up(f, 0)
                        if u == 3:
                            pe.wait_ge(cum_ready, f + 1)
                            gate(f, 1)
                    if u == 4 and attend:
                        if first:
                            pe.wait_ge(rest_ready, 4)
                        else:
                            pe.wait_ge(silu_ready, f * TILES + 1)
                        pe.wait_ge(xv_ready, i + 1)
                        for c in range(NC):
                            last = nc.tensor.matmul(B_V[:, c * P:(c + 1) * P], xv[:, c * P:(c + 1) * P], wv_s[:],
                                                    start=True, stop=True)
                        last.then_inc(v_ps, 1)
                    if experts:
                        if u == 5:
                            pe.wait_ge(hid_ready, f * TILES + 1)
                            up(f, 1)
                            pe.wait_ge(silu_ready, f * TILES + 2)
                            gate(f, 2)
                        if u == 6:
                            if attend:
                                pe.wait_ge(vp_ready, i + 1)
                            else:
                                pe.wait_ge(silu_ready, f * TILES + 1)
                            up(f, 2)
                        if u == 7:
                            pe.wait_ge(hid_ready, f * TILES + 2)
                            gate(f, 3)
                        if u == 8:
                            pe.wait_ge(silu_ready, f * TILES + 3)
                            up(f, 3)
                        if u == 9:
                            pe.wait_ge(hid_ready, f * TILES + 3)
                            gate(f, 4)
                        if u == 10:
                            pe.wait_ge(silu_ready, f * TILES + 4)
                            up(f, 4)
                    if project and 11 <= u <= 14:
                        t = u - 11
                        if t == 0:
                            pe.wait_ge(xb_ready, n + 1)
                            if experts:
                                pe.wait_ge(hid_ready, f * TILES + 4)
                        if t == 1:
                            if experts:
                                pe.wait_ge(silu_ready, f * TILES + 5)
                            else:
                                pe.wait_ge(vp_ready, 1)
                        if t == 2 and experts:
                            pe.wait_ge(hid_ready, f * TILES + 5)
                        if t == 3:
                            pe.wait_ge(rest_ready, n * 4 + 1)
                        project_tile(n, t)
                    if first and u == 15:
                        pe.wait_ge(per_e_ready, 1)
                        pe.wait_ge(rest_ready, n * 4 + 2)
                        nc.tensor.matmul(ps_x[2][:, 0:2 * E], ones[:, 0:P], per_e[:].rearrange("p a e -> p (a e)"),
                                         start=True, stop=True).then_inc(wmean_ps, 1)
                    if experts and u >= 15 and u < 15 + NC:
                        if u == 15:
                            if project:
                                pe.wait_ge(rest_ready, n * 4 + 2)
                            pe.wait_ge(hid_ready, f * TILES + TILES)
                            pe.wait_ge(att_ready, f + 1)
                        out_chunk(f, u - 15)

            pe.wait_ge(xb_ready, 1)
            for t in range(4):
                if t == 3:
                    pe.wait_ge(rest_ready, 1)
                project_tile(0, t)
            iteration(0, True, False, True)
            with pe.Fori(1, NB - 1) as i:
                iteration(i, True, True, True)
            iteration(NB - 1, True, True, False)
            iteration(NB, False, True, False)


def _layouts(v):
    import numpy as np
    a = {k: np.asarray(x) for k, x in v.items()}
    gate = np.concatenate([a['L0_ffn_expert_gate_w'].reshape(E * I, D), a['L0_ffn_shared_gate_w']]).T
    up = np.concatenate([a['L0_ffn_expert_up_w'].reshape(E * I, D), a['L0_ffn_shared_up_w']]).T
    qk = [a[n].reshape(D, NOCT, OCT, F).transpose(0, 1, 3, 2).reshape(D, H * F) for n in ('L0_attn_Wq', 'L0_attn_Wk')]
    wv = a['L0_attn_Wv'].reshape(D, NG, GROUP, DV).transpose(0, 3, 2, 1).reshape(D, H * DV)
    wo = a['L0_attn_Wo'].reshape(NG, GROUP, DV, D).transpose(2, 1, 0, 3).reshape(H * DV, D)
    down = np.concatenate([a['L0_ffn_expert_down_w'].transpose(0, 2, 1).reshape(E * I, D), a['L0_ffn_shared_down_w'].T])
    return {
        'x': a['L0_attn_hidden_states'],
        'w_in': np.concatenate([gate, up, *qk, wv], axis=1),
        'w_v': a['L0_attn_Wv'],
        'w_o': wo,
        'w_down': down.reshape(TILES, P, D).transpose(1, 0, 2),
        'w_route': a['L0_ffn_gate_w'].T,
        'route_bias': a['L0_ffn_lb_bias'],
    }


def kernel(**inputs):
    import numpy as _np
    import concourse.bacc as _bacc
    from concourse import mybir as _mybir
    from concourse.bass_utils import run_bass_kernel_spmd as _run

    nc = _bacc.Bacc("TRN2", target_bir_lowering=False, num_devices=1)
    arrays, args = {}, []
    for name, a in _layouts(inputs).items():
        a = _np.ascontiguousarray(a)
        arrays[f"in_{name}"] = a
        args.append(nc.dram_tensor(f"in_{name}", a.shape, _mybir.dt.from_np(a.dtype), kind="ExternalInput").ap())
    out = nc.dram_tensor("out", (NB, S, D), _mybir.dt.float32, kind="ExternalOutput").ap()
    moe_attention_program(nc, *args, out)
    r = _run(nc, [arrays], core_ids=[0])
    return r.results[0]["out"]
```

```python
import concourse.bass as bass
from concourse import mybir
from contextlib import ExitStack

NB, S, D = 16, 512, 128
H, F, DV = 16, 16, 8
E, I = 8, 64
P = 128
NC = S // P
NT = NB * NC
GROUP = 4
NG = H // GROUP
UNITS = GROUP + 1
SLOTS = NG * UNITS
OCT = 8
NOCT = H // OCT
TILES = E * I // P + 1
HID = TILES * P
PARTS = 3
Q_SLOTS = (0, 1, 2, 0, 1, 0)
K_SLOTS = (0, 0, 0, 1, 1, 2)
KROWS = F * len(Q_SLOTS)
VW = 32
LN_EPS, TOP_EPS, ATT_EPS = 1e-5, 1e-8, 1e-9
GONE = 1e30
MASKS = 2 * GROUP + 1

WQ, WK, WV = 0, H * F, 2 * H * F
GATE = WV + H * DV
UP = GATE + HID
WCOLS = UP + HID


def moe_attention_program(nc, x, w_in, w_v, w_o, w_down, w_route, route_bias, out):
    fp32, bf16, fp32r, i32 = mybir.dt.float32, mybir.dt.bfloat16, mybir.dt.float32r, mybir.dt.int32
    ALU, ACT, AX = mybir.AluOpType, mybir.ActivationFunctionType, mybir.AxisListType
    ctx = ExitStack()
    with ctx:
        def sb(name, shape, dt=fp32):
            return ctx.enter_context(nc.sbuf_tensor(name, shape, dt))

        def sem(name):
            return ctx.enter_context(nc.semaphore(name))

        def scratch(name, shape, dt=fp32):
            return nc.dram_tensor(name, shape, dt, kind="Internal").ap()

        parts_d = [[scratch(f"parts_{n}{o}", [PARTS, F, OCT, S], bf16) for o in range(NOCT)] for n in "qk"]
        sums_d = scratch("sums", [DV + 1, H, S])
        recip_d = scratch("recip", [H, S])

        xnT = sb("xnT", [P, NB * S])
        wts = sb("wts", [P, 2, UNITS, 1024])
        x_all = wts[:].rearrange("p a u n -> p (a u n)")[:, 0:NT * D]
        w_raw = wts[:].rearrange("p a u n -> p (a u n)")[:, NT * D:NT * D + WCOLS]
        q_st = sb("q_stack", [KROWS, NOCT, OCT, S], bf16)
        k_st = sb("k_stack", [KROWS, NOCT, OCT, S], bf16)
        qk_parts = sb("qk_parts", [P, 2 * NOCT, PARTS, S], bf16)
        rest = sb("rest", [P, 2, S])
        w_hi, w_lo = sb("w_hi", [P, WCOLS], fp32r), sb("w_lo", [P, WCOLS], fp32r)
        wv_s, wo_s = sb("wv", [P, H * DV]), sb("wo", [P, D])
        wd_s = sb("wd", [P, TILES, D])
        wr_s, bias_s = sb("wr", [P, E]), sb("route_bias_s", [P, E])
        xa_hi, xa_lo = sb("xa_hi", [P, S], fp32r), sb("xa_lo", [P, S], fp32r)
        xb_hi, xb_lo = sb("xb_hi", [P, S], fp32r), sb("xb_lo", [P, S], fp32r)
        xv = sb("xv", [P, S])
        vp = sb("v_padded", [P, NC, H, VW])
        raw = sb("raw_sums", [P, NG, S])
        num, rec, cum, att = sb("num", [P, S]), sb("rec", [P, S]), sb("cum", [P, S]), sb("att", [P, S])
        den, denr, count = sb("den", [P, S // OCT]), sb("denr", [P, S // OCT]), sb("count", [P, S // OCT])
        count_i = sb("count_i", [P, S // OCT], i32)
        ones = sb("ones", [P, S])
        sil = sb("sil", [P, 2, S])
        hid = sb("hid", [P, TILES, S])
        xres, y = sb("xres", [P, NC, D]), sb("y", [P, NC, D])
        ident, ident_b = sb("ident", [P, P]), sb("ident_b", [P, P], bf16)
        expand = sb("expand", [P, TILES - 1, 2, I], bf16)
        unsel = sb("unsel", [P, NT, E])
        unsel_p = sb("unsel_p", [P, NC, P], bf16)
        unselT = sb("unselT", [P, S], bf16)
        logit = sb("logit", [P, NT, E])
        stat = sb("stat", [P, NT, 6])
        mean, var, rstd, tmp = (sb(n, [P, NT]) for n in ("mean", "var", "rstd", "tmp"))
        m1, m2, t1, sw = (sb(n, [P, NT]) for n in ("m1", "m2", "t1", "sw"))
        order = sb("order", [P, E])
        per_e, wmean = sb("per_e", [P, 2, E]), sb("wmean", [P, 2, E])
        score, one1, one2, rt = (hid[:, n, :].rearrange("p (c e) -> p c e", e=E) for n in range(4))
        xn = num[:].rearrange("p (c d) -> p c d", d=D), cum[:].rearrange("p (c d) -> p c d", d=D)

        x_stage = xv, att
        ps_s = ctx.enter_context(nc.psum_tensor("ps_s", [P, 2, 1024], fp32))
        ps_av = ctx.enter_context(nc.psum_tensor("ps_av", [P, S], fp32))
        ps_x = [ctx.enter_context(nc.psum_tensor(f"ps_x{n}", [P, S], fp32)) for n in range(3)]
        logit_bank = ps_x[2], ps_av
        (B_SEL, B_VT, B_G0, B_U0, B_G1, B_V, B_U1, B_G2, B_U2, B_G3, B_U3, B_G4, B_U4,
         B_Q0, B_K0, B_Q1, B_K1, B_OUT) = (ps_x[n % 3] for n in range(18))
        B_G, B_U, B_P = (B_G0, B_G1, B_G2, B_G3, B_G4), (B_U0, B_U1, B_U2, B_U3, B_U4), (B_Q0, B_K0, B_Q1, B_K1)

        x_in_even, x_in_odd, wp_in, wp_hi, wp_split, xn_pool_step, xn_pool = (sem(n) for n in (
            "x_in_even", "x_in_odd", "wp_in", "wp_hi", "wp_split", "xn_pool_step", "xn_pool"))
        rstd_ready = sem("rstd_ready")
        w_in_sem, xt_ready, xn_ready, stats_step, rstd_step = (sem(n) for n in (
            "w_in_sem", "xt_ready", "xn_ready", "stats_step", "rstd_step"))
        biased = sem("biased")
        var_ready, sqrt_ready, xnT_ready, logits_ps, logits_ready = (sem(n) for n in (
            "var_ready", "sqrt_ready", "xnT_ready", "logits_ps", "logits_ready"))
        scores_e, route_step, per_e_ready, wmean_ps, wd_ready = (sem(n) for n in (
            "scores_e", "route_step", "per_e_ready", "wmean_ps", "wd_ready"))
        consts, const_step, w_split, w_split_hi, unsel_ready = (sem(n) for n in (
            "consts", "const_step", "w_split", "w_split_hi", "unsel_ready"))
        table_ready = sem("table_ready")
        turns = sem("turns")
        scores_ready = sem("scores_ready")
        squares_ready = sem("squares_ready")
        masked = sem("masked")
        av_ready = sem("av_ready")
        raw_ready = sem("raw_ready")
        selT_ps, selT_ready, unsel_p_ready = sem("selT_ps"), sem("selT_ready"), sem("unsel_p_ready")
        vt_ps, cum_ready = sem("vt_ps"), sem("cum_ready")
        gate_ps, up_ps, silu_ready, hid_ready = sem("gate_ps"), sem("up_ps"), sem("silu_ready"), sem("hid_ready")
        v_ps, vp_ready = sem("v_ps"), sem("vp_ready")
        qk_ps, part0_ready, rest_ready, part1_ready, part2_ready = (sem(n) for n in (
            "qk_ps", "part0_ready", "rest_ready", "part1_ready", "part2_ready"))
        xb_hi_ready, xb_ready, xa_hi_ready, xa_ready, xv_ready = (sem(n) for n in (
            "xb_hi_ready", "xb_ready", "xa_hi_ready", "xa_ready", "xv_ready"))
        den_sum, recip_ready, num_sum, att_ready, out_ps, y_ready = (sem(n) for n in (
            "den_sum", "recip_ready", "num_sum", "att_ready", "out_ps", "y_ready"))
        parts_out = [sem(f"parts_out{o}") for o in range(NOCT)]
        stack_in = [sem(f"stack_in{o}") for o in range(NOCT)]
        STACK_DMAS = 9
        xres_in, sums_out, num_in, den_in, recip_out, rec_in, y_out = (sem(n) for n in (
            "xres_in", "sums_out", "num_in", "den_in", "recip_out", "rec_in", "y_out"))

        block = ctx.enter_context(nc.Block())

        def batch_cols(b):
            return bass.ds(b * S, S) if not isinstance(b, int) else slice(b * S, b * S + S)

        def tile_bank(b, t):
            if isinstance(b, int) and b == 0:
                return ps_s[:, t // 2, (t % 2) * S:(t % 2 + 1) * S]
            return B_P[t][:]

        def rows_of(t, b):
            return t[bass.ds(b, 1)].rearrange("a (c p) d -> p (a c) d", p=P)

        @block.sync
        def _(sp):
            sp.dma_start(w_raw[:, 0:GATE], w_in[:, 0:GATE]).then_inc(wp_in, 16)
            q = NB // 4
            for n in range(4):
                x_in = (x_in_even, x_in_odd)[n % 2]
                if n >= 2:
                    sp.wait_ge(x_in, 16)
                sp.dma_start(x_all[:, n * q * NC * D:(n + 1) * q * NC * D].rearrange("p (k d) -> p k d", d=D),
                             x[n * q:(n + 1) * q].rearrange("b (c p) d -> p (b c) d", p=P)).then_inc(x_in, 16)
            for dst, src in ((wr_s[:], w_route), (bias_s[:], route_bias.partition_broadcast(P)),
                             (w_raw[:, GATE:WCOLS], w_in[:, GATE:WCOLS]), (wv_s[:], w_v), (wo_s[:], w_o),
                             (wd_s[:], w_down)):
                sp.dma_start(dst, src).then_inc(w_in_sem, 16)

            def parts_to_dram(b, o):
                sp.wait_ge(part2_ready, b * 4 + 2 * o + 2)
                sp.sem_inc(turns, 1)
                if not isinstance(b, int) or b > 0:
                    sp.wait_ge(stack_in[o], b * (16 * STACK_DMAS))
                for n in range(2):
                    sp.dma_start(parts_d[n][o].rearrange("r f h s -> (f h) r s"),
                                 qk_parts[:, 2 * o + n]).then_inc(parts_out[o], 16)

            def stacks_from_dram(b, o):
                sp.wait_ge(parts_out[o], b * 32 + 32)
                if not isinstance(b, int) or b > 0:
                    sp.wait_ge(scores_ready, (b - 1) * SLOTS + 2 * UNITS * (o + 1))
                q_rows = parts_d[0][o].rearrange("r f h s -> (r f) (h s)")
                k_rows = parts_d[1][o].rearrange("r f h s -> (r f) (h s)")
                row = 0
                for n in (3, 2, 1):
                    sp.dma_start(q_st[row:row + n * F, o].rearrange("p h s -> p (h s)"),
                                 q_rows[0:n * F]).then_inc(stack_in[o], 16)
                    row += n * F
                for r, part in enumerate(K_SLOTS):
                    sp.dma_start(k_st[r * F:(r + 1) * F, o].rearrange("p h s -> p (h s)"),
                                 k_rows[part * F:(part + 1) * F]).then_inc(stack_in[o], 16)

            def iteration(i, attend, experts, project):
                f, n = i - 1, i + 1
                if attend:
                    stacks_from_dram(i, 1)
                if experts:
                    if not isinstance(f, int) or f > 0:
                        sp.wait_ge(y_ready, f)
                        sp.sem_inc(turns, 1)
                    sp.dma_start(xres[:], rows_of(x, f)).then_inc(xres_in, 16)
                    sp.wait_ge(raw_ready, f * NG + NG)
                    for j in range(GROUP):
                        sp.dma_start(sums_d[:, j * NG:(j + 1) * NG, :],
                                     raw[32 * j:32 * j + DV + 1]).then_inc(sums_out, 16)
                    sp.wait_ge(sums_out, f * (16 * GROUP) + 16 * GROUP)
                    sp.dma_start(den[:], sums_d[DV].rearrange("h (k s) -> (h k) s", s=S // OCT)).then_inc(den_in, 16)
                    if not isinstance(f, int) or f > 0:
                        sp.wait_ge(num_sum, f)
                    sp.dma_start(num[:], sums_d[0:DV].rearrange("d h s -> (d h) s")).then_inc(num_in, 16)
                    sp.wait_ge(recip_ready, f + 1)
                    sp.dma_start(recip_d.rearrange("h (k s) -> (h k) s", s=S // OCT), denr[:]).then_inc(recip_out, 16)
                    sp.wait_ge(recip_out, f * 16 + 16)
                    if not isinstance(f, int) or f > 0:
                        sp.wait_ge(att_ready, f)
                    for d in range(DV):
                        sp.dma_start(rec[d * H:(d + 1) * H, :], recip_d).then_inc(rec_in, 16)
                if project:
                    parts_to_dram(n, 0)
                    stacks_from_dram(n, 0)
                    parts_to_dram(n, 1)
                if experts:
                    sp.wait_ge(y_ready, f + 1)
                    sp.sem_inc(turns, 1)
                    sp.dma_start(rows_of(out, f), y[:]).then_inc(y_out, 16)

            parts_to_dram(0, 0)
            stacks_from_dram(0, 0)
            parts_to_dram(0, 1)
            iteration(0, True, False, True)
            iteration(1, True, True, True)
            with sp.Fori(2, NB - 1) as i:
                iteration(i, True, True, True)
            iteration(NB - 1, True, True, False)
            iteration(NB, False, True, False)
            sp.wait_ge(y_out, 16 * NB)

        @block.gpsimd
        def _(pool):
            nc.gpsimd.memset(ident[:], 0.0).then_inc(const_step, 1)
            nc.gpsimd.memset(ident_b[:], 0.0).then_inc(const_step, 1)
            nc.gpsimd.memset(expand[:], GONE).then_inc(const_step, 1)
            nc.gpsimd.memset(vp[:], 0.0).then_inc(const_step, 1)
            nc.gpsimd.memset(unsel_p[:], 0.0).then_inc(const_step, 1)
            nc.gpsimd.memset(ones[:], 1.0).then_inc(const_step, 1)
            pool.wait_ge(const_step, 6)
            for m in (ident, ident_b):
                nc.gpsimd.affine_select(out=m[:], in_=m[:], compare_op=ALU.not_equal, fill=1.0, base=0,
                                        pattern=[[-1, P]], channel_multiplier=1).then_inc(consts, 1)
            nc.gpsimd.affine_select(out=expand[:], in_=expand[:], compare_op=ALU.is_equal, fill=0.0, base=0,
                                    pattern=[[-2, TILES - 1], [-1, 2], [0, I]], channel_multiplier=1).then_inc(consts, 1)
            nc.gpsimd.memset(vp[:, :, :, DV:DV + 1], 1.0).then_inc(consts, 1)
            nc.gpsimd.iota(order[:], pattern=[[-1, E]], base=E, channel_multiplier=0,
                           allow_small_or_imprecise_dtypes=True).then_inc(consts, 1)
            nc.gpsimd.iota(count_i[:], pattern=[[1, S // OCT]], base=0, channel_multiplier=S // OCT).then_inc(consts, 1)

            def mask(b, u):
                g, j = divmod(u, UNITS)
                w = wts[:, g % 2, j, :]
                pool.wait_ge(squares_ready, b * SLOTS + u + 1)
                pool.sem_inc(turns, 1)
                keep = dict(compare_op=ALU.is_ge, fill=0.0, base=0, channel_multiplier=-1)
                if j < GROUP:
                    v = w.rearrange("p (a n) -> p a n", a=2)[:, :, 0:P]
                    nc.gpsimd.affine_select(out=v, in_=v, pattern=[[0, 2], [1, P]], **keep).then_inc(masked, 1)
                    v = w[:, 1024 - P:1024]
                    nc.gpsimd.affine_select(out=v, in_=v, pattern=[[1, P]], **keep).then_inc(masked, 1)
                else:
                    v = w.rearrange("p (a n) -> p a n", a=GROUP)[:, :, 0:P]
                    nc.gpsimd.affine_select(out=v, in_=v, pattern=[[0, GROUP], [1, P]], **keep).then_inc(masked, 1)

            def choose(b):
                if not isinstance(b, int) or b > 0:
                    pool.wait_ge(selT_ps, b)
                    pool.sem_inc(turns, 1)
                chunks = bass.ds(b * NC, NC) if not isinstance(b, int) else slice(b * NC, b * NC + NC)
                nc.gpsimd.tensor_copy(unsel_p[:, :, 0:E], unsel[:, chunks, :]).then_inc(unsel_p_ready, 1)

            def normalise(k):
                if isinstance(k, int):
                    pool.wait_ge(rstd_ready, 1)
                else:
                    pool.wait_ge(xt_ready, k * 2)
                    pool.sem_inc(turns, 1)
                for par in range(2):
                    row = (k * 2 + par) * NC + NC - 1
                    cols, one = (bass.ds(row * D, D), bass.ds(row, 1)) if not isinstance(k, int) else (
                        slice(row * D, row * D + D), slice(row, row + 1))
                    to = xn[par][:, NC - 1, :]
                    nc.gpsimd.tensor_tensor(to, x_all[:, cols], mean[:, one].to_broadcast([P, D]),
                                            ALU.subtract).then_inc(xn_pool_step, 1)
                    pool.wait_ge(xn_pool_step, k * 2 + par + 1)
                    pool.sem_inc(turns, 1)
                    nc.gpsimd.tensor_tensor(to, to, rstd[:, one].to_broadcast([P, D]), ALU.mult).then_inc(xn_pool, 1)

            normalise(0)
            with pool.Fori(1, NB // 2) as k:
                normalise(k)

            def iteration(i):
                for u in range(SLOTS):
                    mask(i, u)
                    if u == SLOTS // 2:
                        choose(i)

            for u in range(SLOTS):
                mask(0, u)
            pool.wait_ge(unsel_ready, 1)
            choose(0)
            with pool.Fori(1, NB) as i:
                iteration(i)

        @block.scalar
        def _(act):
            act.wait_ge(var_ready, 1)
            nc.scalar.activation(tmp[:], var[:], ACT.Sqrt).then_inc(sqrt_ready, 1)

            def transposed(k):
                for par in range(2):
                    b = k * 2 + par
                    act.wait_ge(xt_ready, b + 1)
                    nc.scalar.activation(xnT[:, batch_cols(b)], ps_x[par][:], ACT.Copy).then_inc(xnT_ready, 1)
                    nc.scalar.activation(x_stage[par][:], ps_x[par][:], ACT.Copy).then_inc(xnT_ready, 1)
                for par in range(2):
                    b = k * 2 + par
                    act.wait_ge(logits_ps, b + 1)
                    rows = bass.ds(b * NC, NC) if not isinstance(b, int) else slice(b * NC, b * NC + NC)
                    nc.scalar.activation(logit[:, rows, :], logit_bank[par][:, 0:NC * E].rearrange(
                        "p (c e) -> p c e", e=E), ACT.Copy).then_inc(logits_ready, 1)

            def square(b, u):
                g, j = divmod(u, UNITS)
                act.wait_ge(scores_ready, b * SLOTS + u + 1)
                if j == 0 and not (isinstance(b, int) and b == 0 and g < 2):
                    act.wait_ge(av_ready, b * NG + g - 1)
                nc.scalar.activation(wts[:, g % 2, j, :], ps_s[:, u % 2, :], ACT.Square, bias=1.0,
                                     scale=0.25).then_inc(squares_ready, 1)

            def sums_out_of_psum(b, g):
                act.wait_ge(av_ready, b * NG + g + 1)
                if g == 0 and not (isinstance(b, int) and b == 0):
                    act.wait_ge(sums_out, b * (16 * GROUP))
                nc.scalar.activation(raw[:, g, :], ps_av[:], ACT.Copy).then_inc(raw_ready, 1)

            def silu(b, j):
                act.wait_ge(gate_ps, b * TILES + j + 1)
                if j >= 2:
                    act.wait_ge(hid_ready, b * TILES + j - 1)
                elif not (isinstance(b, int) and b == 0):
                    act.wait_ge(hid_ready, b * TILES)
                nc.scalar.activation(sil[:, j % 2, :], B_G[j][:], ACT.Silu).then_inc(silu_ready, 1)

            def part0(b, t):
                act.wait_ge(qk_ps, b * 4 + t + 1)
                if not (isinstance(b, int) and b == 0):
                    act.wait_ge(parts_out[t // 2], b * 32)
                nc.scalar.activation(qk_parts[:, t, 0, :], tile_bank(b, t), ACT.Copy).then_inc(part0_ready, 1)

            def v_out(b):
                act.wait_ge(v_ps, b + 1)
                if not (isinstance(b, int) and b == 0):
                    act.wait_ge(av_ready, b * NG)
                else:
                    act.wait_ge(consts, 6)
                nc.scalar.activation(vp[:].rearrange("p c h w -> p (c h) w")[:, :, 0:DV],
                                     B_V[:].rearrange("p (k d) -> p k d", d=DV), ACT.Copy).then_inc(vp_ready, 1)

            def iteration(i, attend, experts, project):
                f, n = i - 1, i + 1
                for u in range(SLOTS):
                    if attend:
                        square(i, u)
                    if u == 0 and experts:
                        act.wait_ge(selT_ps, f + 1)
                        nc.scalar.activation(unselT[:], B_SEL[:], ACT.Copy).then_inc(selT_ready, 1)
                    if experts and u in (1, 3, 5, 7, 9):
                        silu(f, (u - 1) // 2)
                    if u == 4:
                        if experts:
                            sums_out_of_psum(f, NG - 1)
                        if attend:
                            v_out(i)
                    if attend and u in (9, 14, 19):
                        sums_out_of_psum(i, u // UNITS - 1)
                    if project and 11 <= u <= 14:
                        part0(n, u - 11)

            transposed(0)
            transposed(1)
            for t in range(4):
                part0(0, t)
            with act.Fori(2, NB // 2) as k:
                transposed(k)
            act.wait_ge(biased, 1)
            nc.scalar.activation(score, logit[:], ACT.Sigmoid).then_inc(scores_e, 1)
            act.wait_ge(scores_e, 1)
            nc.scalar.activation(sil[:, 0, 0:1], ones[:, 0:1], ACT.Silu).then_inc(table_ready, 1)
            act.wait_ge(w_split, 1)
            act.wait_ge(xn_ready, NB * (NC - 1))
            act.wait_ge(xn_pool, NB)
            iteration(0, True, False, True)
            iteration(1, True, True, True)
            with act.Fori(2, NB - 1) as i:
                iteration(i, True, True, True)
            iteration(NB - 1, True, True, False)
            iteration(NB, False, True, False)

        @block.vector
        def _(dve):
            steps = {}

            def step(ins, s):
                steps[s.name] = steps.get(s.name, 0) + 1
                ins.then_inc(s, 1)
                dve.wait_ge(s, steps[s.name])

            def split_weights(cols, hi_sem, lo_sem):
                nc.vector.tensor_copy(w_hi[:, cols], w_raw[:, cols]).then_inc(hi_sem, 1)
                dve.wait_ge(hi_sem, 1)
                nc.vector.tensor_tensor(w_lo[:, cols], w_raw[:, cols], w_hi[:, cols].bitcast(fp32),
                                        ALU.subtract).then_inc(lo_sem, 1)

            dve.wait_ge(wp_in, 16)
            split_weights(slice(0, GATE), wp_hi, wp_split)
            QR = NT // 4
            with dve.Fori(0, 2) as k:
                for par in range(2):
                    dve.wait_ge((x_in_even, x_in_odd)[par], k * 16 + 16)
                    for n in range(QR):
                        c = k * (2 * QR) + (par * QR + n)
                        nc.vector.bn_stats(stat[:, bass.ds(c, 1), :].rearrange("p a n -> p (a n)"),
                                           x_all[:, bass.ds(c * D, D)]).then_inc(stats_step, 1)
            dve.wait_ge(stats_step, NT)
            nc.vector.tensor_tensor(m1[:], stat[:, :, 1], stat[:, :, 4], ALU.subtract).then_inc(rstd_step, 1)
            nc.vector.tensor_tensor(m2[:], stat[:, :, 2], stat[:, :, 5], ALU.add).then_inc(rstd_step, 1)
            nc.vector.tensor_tensor(mean[:], stat[:, :, 1], stat[:, :, 4], ALU.add).then_inc(rstd_step, 1)
            steps[rstd_step.name] = 3
            dve.wait_ge(rstd_step, 3)
            step(nc.vector.scalar_tensor_tensor(m1[:], m1[:], 0.25, m1[:], ALU.mult, ALU.mult), rstd_step)
            step(nc.vector.scalar_tensor_tensor(var[:], m2[:], 1.0 / D, m1[:], ALU.mult, ALU.add), rstd_step)
            nc.vector.tensor_scalar(var[:], var[:], LN_EPS, None, ALU.add).then_inc(var_ready, 1)
            step(nc.vector.tensor_scalar(mean[:], mean[:], 0.5, None, ALU.mult), rstd_step)
            dve.wait_ge(sqrt_ready, 1)
            step(nc.vector.reciprocal(rstd[:], tmp[:]), rstd_step)
            step(nc.vector.tensor_tensor(t1[:], rstd[:], rstd[:], ALU.mult), rstd_step)
            step(nc.vector.scalar_tensor_tensor(t1[:], t1[:], -0.5, var[:], ALU.mult, ALU.mult), rstd_step)
            nc.vector.scalar_tensor_tensor(rstd[:], t1[:], 1.5, rstd[:], ALU.add, ALU.mult).then_inc(rstd_ready, 1)
            dve.wait_ge(rstd_ready, 1)

            def normalise(k):
                if not isinstance(k, int) or k > 0:
                    dve.wait_ge(xt_ready, k * 2)
                for par in range(2):
                    for c in range(NC - 1):
                        row = (k * 2 + par) * NC + c
                        cols, one = (bass.ds(row * D, D), bass.ds(row, 1)) if not isinstance(k, int) else (
                            slice(row * D, row * D + D), slice(row, row + 1))
                        nc.vector.tensor_scalar(xn[par][:, c, :], x_all[:, cols], mean[:, one], rstd[:, one],
                                                ALU.subtract, ALU.mult).then_inc(xn_ready, 1)

            def split_x(b, hi, lo, hi_sem, lo_sem):
                nc.vector.tensor_scalar(hi[:], xnT[:, batch_cols(b)], 1.0, None, ALU.mult).then_inc(hi_sem, 1)
                dve.wait_ge(hi_sem, b + 1)
                nc.vector.tensor_tensor(lo[:], xnT[:, batch_cols(b)], hi[:].bitcast(fp32),
                                        ALU.subtract).then_inc(lo_sem, 1)

            def split_tile(b, t):
                r = rest[:, t % 2, :]
                dve.wait_ge(part0_ready, b * 4 + t + 1)
                if t >= 2:
                    dve.wait_ge(part2_ready, b * 4 + t - 1)
                elif not (isinstance(b, int) and b == 0):
                    dve.wait_ge(part2_ready, b * 4 + t - 1)
                nc.vector.tensor_tensor(r, tile_bank(b, t), qk_parts[:, t, 0, :], ALU.subtract).then_inc(rest_ready, 1)
                dve.wait_ge(rest_ready, b * 4 + t + 1)
                nc.vector.tensor_copy(qk_parts[:, t, 1, :], r).then_inc(part1_ready, 1)
                dve.wait_ge(part1_ready, b * 4 + t + 1)
                nc.vector.tensor_tensor(qk_parts[:, t, 2, :], r, qk_parts[:, t, 1, :],
                                        ALU.subtract).then_inc(part2_ready, 1)

            def hidden(b, j):
                dve.wait_ge(up_ps, b * TILES + j + 1)
                dve.wait_ge(silu_ready, b * TILES + j + 1)
                if j == 0 and not (isinstance(b, int) and b == 0):
                    dve.wait_ge(out_ps, b)
                nc.vector.tensor_tensor(hid[:, j, :], B_U[j][:], sil[:, j % 2, :], ALU.mult).then_inc(hid_ready, 1)

            def copy_xv(b):
                if isinstance(b, int) and b == 0:
                    dve.wait_ge(logits_ps, NB)
                else:
                    dve.wait_ge(v_ps, b)
                nc.vector.tensor_scalar(xv[:], xnT[:, batch_cols(b)], 1.0, None, ALU.mult).then_inc(xv_ready, 1)

            def routing():
                dve.wait_ge(scores_e, 1)
                dve.wait_ge(consts, 6)
                wide = [P, NT, E]
                o = order[:].unsqueeze(1).to_broadcast(wide)

                def b3(t):
                    return t[:].unsqueeze(2).to_broadcast(wide)

                def best(src, m, one):
                    step(nc.vector.tensor_reduce(m[:], src, AX.X, ALU.max), route_step)
                    step(nc.vector.tensor_tensor(rt, src, b3(m), ALU.is_equal), route_step)
                    step(nc.vector.tensor_tensor(rt, rt, o, ALU.mult), route_step)
                    step(nc.vector.tensor_reduce(t1[:], rt, AX.X, ALU.max), route_step)
                    step(nc.vector.tensor_tensor(one, rt, b3(t1), ALU.is_equal), route_step)

                best(score, m1, one1)
                step(nc.vector.scalar_tensor_tensor(score, one1, -4.0, score, ALU.mult, ALU.add), route_step)
                best(score, m2, one2)
                step(nc.vector.tensor_tensor(rt, one1, one2, ALU.add), route_step)
                nc.vector.tensor_scalar(unsel[:], rt, -1.0, None, ALU.add).then_inc(unsel_ready, 1)
                step(nc.vector.tensor_reduce(per_e[:, 1, :], rt.rearrange("p c e -> p e c"), AX.X, ALU.add), route_step)
                step(nc.vector.scalar_tensor_tensor(sw[:], m1[:], TOP_EPS, m2[:], ALU.add, ALU.add), route_step)
                step(nc.vector.reciprocal(sw[:], sw[:]), route_step)
                step(nc.vector.tensor_tensor(m1[:], m1[:], sw[:], ALU.mult), route_step)
                step(nc.vector.tensor_tensor(m2[:], m2[:], sw[:], ALU.mult), route_step)
                step(nc.vector.tensor_tensor(one1, one1, b3(m1), ALU.mult), route_step)
                step(nc.vector.tensor_tensor(one2, one2, b3(m2), ALU.mult), route_step)
                step(nc.vector.tensor_tensor(rt, one1, one2, ALU.add), route_step)
                nc.vector.tensor_reduce(per_e[:, 0, :], rt.rearrange("p c e -> p e c"), AX.X, ALU.add).then_inc(per_e_ready, 1)

            def mean_weights():
                dve.wait_ge(wmean_ps, 1)
                step(nc.vector.tensor_copy(wmean[:], ps_x[2][:, 0:2 * E].rearrange("p (a e) -> p a e", a=2)), route_step)
                step(nc.vector.tensor_scalar(wmean[:, 1, :], wmean[:, 1, :], 1.0, None, ALU.max), route_step)
                step(nc.vector.reciprocal(wmean[:, 1, :], wmean[:, 1, :]), route_step)
                step(nc.vector.tensor_tensor(wmean[:, 0, :], wmean[:, 0, :], wmean[:, 1, :], ALU.mult), route_step)
                dve.wait_ge(w_in_sem, 16 * 6)
                for e in range(E):
                    r = slice(I * (e % 2), I * (e % 2) + I)
                    nc.vector.tensor_scalar(wd_s[r, e // 2, :], wd_s[r, e // 2, :], wmean[r, 0, e:e + 1], None,
                                            ALU.mult).then_inc(wd_ready, 1)
                step(nc.vector.tensor_single_scalar(count_i[:], count_i[:], S - 1, ALU.bitwise_and), route_step)
                step(nc.vector.tensor_copy(count[:], count_i[:]), route_step)
                step(nc.vector.tensor_scalar(count[:], count[:], 1.0, None, ALU.add), route_step)

            def iteration(i, attend, experts, project):
                f, n = i - 1, i + 1
                if project:
                    dve.wait_ge(qk_ps, n * 4)
                    split_x(n, xb_hi, xb_lo, xb_hi_ready, xb_ready)
                if experts:
                    dve.wait_ge(vt_ps, f + 1)
                    nc.vector.tensor_tensor_scan(cum[:], ones[:], B_VT[:], 0.0, ALU.mult, ALU.add).then_inc(cum_ready, 1)
                    for j in range(4):
                        hidden(f, j)
                    dve.wait_ge(den_in, f * 16 + 16)
                    if not isinstance(f, int) or f > 0:
                        dve.wait_ge(recip_out, f * 16)
                    nc.vector.scalar_tensor_tensor(den[:], den[:], 2 * ATT_EPS, count[:], ALU.add,
                                                   ALU.add).then_inc(den_sum, 1)
                    dve.wait_ge(den_sum, f + 1)
                    nc.vector.reciprocal(denr[:], den[:]).then_inc(recip_ready, 1)
                    hidden(f, 4)
                if not experts:
                    routing()
                if attend:
                    if experts:
                        dve.wait_ge(up_ps, f * TILES + TILES)
                    split_x(i, xa_hi, xa_lo, xa_hi_ready, xa_ready)
                if project:
                    split_tile(n, 0)
                    split_tile(n, 1)
                if experts:
                    dve.wait_ge(num_in, f * 16 + 16)
                    dve.wait_ge(cum_ready, f + 1)
                    nc.vector.tensor_tensor(cum[:], num[:], cum[:], ALU.add).then_inc(num_sum, 1)
                    dve.wait_ge(num_sum, f + 1)
                    dve.wait_ge(rec_in, f * (16 * DV) + 16 * DV)
                    if not isinstance(f, int) or f > 0:
                        dve.wait_ge(out_ps, f)
                    nc.vector.tensor_tensor(att[:], cum[:], rec[:], ALU.mult).then_inc(att_ready, 1)
                if project:
                    split_tile(n, 2)
                    split_tile(n, 3)
                    copy_xv(n)
                if not experts:
                    mean_weights()
                if experts:
                    dve.wait_ge(out_ps, f + 1)
                    dve.wait_ge(xres_in, f * 16 + 16)
                    if not isinstance(f, int) or f > 0:
                        dve.wait_ge(y_out, f * 16)
                    nc.vector.tensor_tensor(y[:], B_OUT[:].rearrange("p (c d) -> p c d", d=D), xres[:],
                                            ALU.add).then_inc(y_ready, 1)

            normalise(0)
            normalise(1)
            dve.wait_ge(xnT_ready, 1)
            split_x(0, xb_hi, xb_lo, xb_hi_ready, xb_ready)
            normalise(2)
            for t in range(4):
                split_tile(0, t)
            dve.wait_ge(w_in_sem, 16 * 6)
            split_weights(slice(GATE, WCOLS), w_split_hi, w_split)
            with dve.Fori(3, NB // 2) as k:
                normalise(k)
            dve.wait_ge(logits_ready, NB)
            nc.vector.tensor_tensor(logit[:], logit[:], bias_s[:].unsqueeze(1).to_broadcast([P, NT, E]),
                                    ALU.add).then_inc(biased, 1)
            dve.wait_ge(xnT_ready, 2 * NB)
            copy_xv(0)
            iteration(0, True, False, True)
            iteration(1, True, True, True)
            with dve.Fori(2, NB - 1) as i:
                iteration(i, True, True, True)
            iteration(NB - 1, True, True, False)
            iteration(NB, False, True, False)

        @block.tensor
        def _(pe):
            pe.wait_ge(consts, 6)

            def transpose_pair(k):
                for par in range(2):
                    b = k * 2 + par
                    pe.wait_ge(xn_ready, b * (NC - 1) + NC - 1)
                    pe.wait_ge(xn_pool, b + 1)
                    for c in range(NC):
                        last = nc.tensor.transpose(ps_x[par][:, c * P:(c + 1) * P], xn[par][:, c, :], ident[:])
                    last.then_inc(xt_ready, 1)
                for par in range(2):
                    b = k * 2 + par
                    pe.wait_ge(xnT_ready, b * 2 + 2)
                    if isinstance(k, int) and k == 0:
                        pe.wait_ge(w_in_sem, 16 * 6)
                    else:
                        pe.wait_ge(logits_ready, k * 2)
                    for c in range(NC):
                        last = nc.tensor.matmul(logit_bank[par][:, c * E:(c + 1) * E],
                                                x_stage[par][:, c * P:(c + 1) * P], wr_s[:], start=True, stop=True)
                    last.then_inc(logits_ps, 1)

            def three(bank, col, hi, lo, stop=True):
                nc.tensor.matmul(bank, w_hi[:, col:col + P], hi[:], start=True, stop=False)
                nc.tensor.matmul(bank, w_lo[:, col:col + P], hi[:], start=False, stop=False)
                return nc.tensor.matmul(bank, w_hi[:, col:col + P], lo[:], start=False, stop=stop)

            def project_tile(b, t):
                o, n = divmod(t, 2)
                col = (WQ, WK)[n] + o * P
                three(tile_bank(b, t), col, xb_hi, xb_lo).then_inc(qk_ps, 1)

            def scores(b, u):
                g, j = divmod(u, UNITS)
                o = g // 2
                if not (isinstance(b, int) and b == 0 and u < 2):
                    pe.wait_ge(squares_ready, b * SLOTS + u - 1)
                if u % (2 * UNITS) == 0:
                    pe.wait_ge(stack_in[o], b * (16 * STACK_DMAS) + 16 * STACK_DMAS)

                def chunk(head, key, dst):
                    h = head % OCT
                    return nc.tensor.matmul(dst, k_st[:, o, h, key * P:(key + 1) * P],
                                            q_st[:, o, h, key * P:S], start=True, stop=True)
                ps = ps_s[:, u % 2, :]
                if j < GROUP:
                    chunk(g * GROUP + j, 0, ps[:, 0:512])
                    chunk(g * GROUP + j, 1, ps[:, 512:896])
                    last = chunk(g * GROUP + j, 3, ps[:, 896:1024])
                else:
                    for jj in range(GROUP):
                        last = chunk(g * GROUP + jj, 2, ps[:, jj * 256:(jj + 1) * 256])
                last.then_inc(scores_ready, 1)

            AV = ((0, 0, 512), (1, 512, 896), (3, 896, 1024), (2, None, None))

            def weighted(b, g, n):
                key, lo, hi = AV[n]
                if n == 0:
                    pe.wait_ge(masked, b * (NG * MASKS) + (g + 1) * MASKS)
                    if not (isinstance(b, int) and b == 0 and g == 0):
                        pe.wait_ge(raw_ready, b * NG + g)
                    if g == 0:
                        pe.wait_ge(vp_ready, b + 1)
                for j in range(GROUP):
                    w = wts[:, g % 2, j, lo:hi] if key != 2 else wts[:, g % 2, GROUP, j * 256:(j + 1) * 256]
                    last = nc.tensor.matmul(ps_av[32 * j:32 * j + VW, key * P:S], vp[:, key, g * GROUP + j, :], w,
                                            start=(n == 0), stop=(n == 3))
                if n == 3:
                    last.then_inc(av_ready, 1)

            def gate(b, j):
                last = three(B_G[j][:], GATE + j * P, xa_hi, xa_lo, stop=(j == TILES - 1))
                if j < TILES - 1:
                    if j == 0:
                        pe.wait_ge(selT_ready, b + 1)
                    last = nc.tensor.matmul(B_G[j][:], expand[:, j].rearrange("p a i -> p (a i)"), unselT[:],
                                            start=False, stop=True)
                last.then_inc(gate_ps, 1)

            def up(b, j):
                three(B_U[j][:], UP + j * P, xa_hi, xa_lo).then_inc(up_ps, 1)

            def down_chunk(b, c):
                tok = slice(c * P, (c + 1) * P)
                for j in range(TILES):
                    nc.tensor.matmul(B_OUT[:, tok], hid[:, j, tok], wd_s[:, j, :], start=(c == 0 and j == 0),
                                     stop=False, skip_group_check=True)

            def attention_out(b):
                pe.wait_ge(att_ready, b + 1)
                for c in range(NC):
                    tok = slice(c * P, (c + 1) * P)
                    last = nc.tensor.matmul(B_OUT[:, tok], att[:, tok], wo_s[:], start=False, stop=(c == NC - 1),
                                            skip_group_check=True)
                last.then_inc(out_ps, 1)

            def iteration(i, attend, experts, project):
                f, n = i - 1, i + 1
                first = isinstance(i, int) and i == 0
                final = isinstance(i, int) and i == NB
                for u in range(SLOTS):
                    g, j = divmod(u, UNITS)
                    if attend:
                        scores(i, u)
                    if j > 0:
                        if g == 0 and experts:
                            weighted(f, NG - 1, j - 1)
                        elif g > 0 and attend:
                            weighted(i, g - 1, j - 1)
                    if experts:
                        if u == 0:
                            pe.wait_ge(unsel_p_ready, f + 1)
                            if final:
                                pe.wait_ge(hid_ready, f * TILES)
                            else:
                                pe.wait_ge(rest_ready, i * 4 + 3)
                            for c in range(NC):
                                last = nc.tensor.matmul(B_SEL[:, c * P:(c + 1) * P], unsel_p[:, c, :], ident_b[:],
                                                        start=True, stop=True)
                            last.then_inc(selT_ps, 1)
                            pe.wait_ge(xa_ready, f + 1)
                            if not final:
                                pe.wait_ge(rest_ready, i * 4 + 4)
                            three(B_VT[:], WV, xa_hi, xa_lo).then_inc(vt_ps, 1)
                        if u == 1:
                            pe.wait_ge(y_ready, f)
                            pe.wait_ge(wd_ready, E)
                            gate(f, 0)
                        if u == 2:
                            pe.wait_ge(selT_ready, f + 1)
                            up(f, 0)
                        if u == 3:
                            pe.wait_ge(cum_ready, f + 1)
                            gate(f, 1)
                    if u == 4 and attend:
                        if not first:
                            pe.wait_ge(silu_ready, f * TILES + 1)
                        pe.wait_ge(xv_ready, i + 1)
                        for c in range(NC):
                            last = nc.tensor.matmul(B_V[:, c * P:(c + 1) * P], xv[:, c * P:(c + 1) * P], wv_s[:],
                                                    start=True, stop=True)
                        last.then_inc(v_ps, 1)
                    if experts:
                        if u == 5:
                            pe.wait_ge(hid_ready, f * TILES + 1)
                            up(f, 1)
                            pe.wait_ge(silu_ready, f * TILES + 2)
                            gate(f, 2)
                        if u == 6:
                            if attend:
                                pe.wait_ge(vp_ready, i + 1)
                            else:
                                pe.wait_ge(silu_ready, f * TILES + 1)
                            up(f, 2)
                        if u == 7:
                            pe.wait_ge(hid_ready, f * TILES + 2)
                            gate(f, 3)
                        if u == 8:
                            pe.wait_ge(silu_ready, f * TILES + 3)
                            up(f, 3)
                        if u == 9:
                            pe.wait_ge(hid_ready, f * TILES + 3)
                            gate(f, 4)
                        if u == 10:
                            pe.wait_ge(silu_ready, f * TILES + 4)
                            up(f, 4)
                    if project and 11 <= u <= 14:
                        t = u - 11
                        if t == 0:
                            pe.wait_ge(xb_ready, n + 1)
                            if experts:
                                pe.wait_ge(hid_ready, f * TILES + 4)
                        if t == 1:
                            if experts:
                                pe.wait_ge(silu_ready, f * TILES + 5)
                            else:
                                pe.wait_ge(vp_ready, 1)
                        if t == 2 and experts:
                            pe.wait_ge(hid_ready, f * TILES + 5)
                        if t == 3:
                            pe.wait_ge(rest_ready, n * 4 + 1)
                        project_tile(n, t)
                    if first and u == 15:
                        pe.wait_ge(per_e_ready, 1)
                        pe.wait_ge(rest_ready, n * 4 + 2)
                        nc.tensor.matmul(ps_x[2][:, 0:2 * E], ones[:, 0:P], per_e[:].rearrange("p a e -> p (a e)"),
                                         start=True, stop=True).then_inc(wmean_ps, 1)
                    if experts and u >= 15 and u < 15 + NC:
                        if u == 15:
                            if project:
                                pe.wait_ge(rest_ready, n * 4 + 2)
                            pe.wait_ge(hid_ready, f * TILES + TILES)
                        down_chunk(f, u - 15)
                    if experts and u == SLOTS - 1:
                        attention_out(f)

            transpose_pair(0)
            transpose_pair(1)
            pe.wait_ge(wp_split, 1)
            pe.wait_ge(xb_ready, 1)
            for t in range(4):
                project_tile(0, t)
            with pe.Fori(2, NB // 2) as k:
                transpose_pair(k)
            pe.wait_ge(rest_ready, 4)
            pe.wait_ge(logits_ready, NB)
            iteration(0, True, False, True)
            iteration(1, True, True, True)
            with pe.Fori(2, NB - 1) as i:
                iteration(i, True, True, True)
            iteration(NB - 1, True, True, False)
            iteration(NB, False, True, False)


def _layouts(v):
    import numpy as np
    a = {k: np.asarray(x) for k, x in v.items()}
    gate = np.concatenate([a['L0_ffn_expert_gate_w'].reshape(E * I, D), a['L0_ffn_shared_gate_w']]).T
    up = np.concatenate([a['L0_ffn_expert_up_w'].reshape(E * I, D), a['L0_ffn_shared_up_w']]).T
    qk = [a[n].reshape(D, NOCT, OCT, F).transpose(0, 1, 3, 2).reshape(D, H * F) for n in ('L0_attn_Wq', 'L0_attn_Wk')]
    wv = a['L0_attn_Wv'].reshape(D, NG, GROUP, DV).transpose(0, 3, 2, 1).reshape(D, H * DV)
    wo = a['L0_attn_Wo'].reshape(NG, GROUP, DV, D).transpose(2, 1, 0, 3).reshape(H * DV, D)
    down = np.concatenate([a['L0_ffn_expert_down_w'].transpose(0, 2, 1).reshape(E * I, D), a['L0_ffn_shared_down_w'].T])
    return {
        'x': a['L0_attn_hidden_states'],
        'w_in': np.concatenate([*qk, wv, gate, up], axis=1),
        'w_v': a['L0_attn_Wv'],
        'w_o': wo,
        'w_down': down.reshape(TILES, P, D).transpose(1, 0, 2),
        'w_route': a['L0_ffn_gate_w'].T,
        'route_bias': a['L0_ffn_lb_bias'],
    }


def kernel(**inputs):
    import numpy as _np
    import concourse.bacc as _bacc
    from concourse import mybir as _mybir
    from concourse.bass_utils import run_bass_kernel_spmd as _run

    nc = _bacc.Bacc("TRN2", target_bir_lowering=False, num_devices=1)
    arrays, args = {}, []
    for name, a in _layouts(inputs).items():
        a = _np.ascontiguousarray(a)
        arrays[f"in_{name}"] = a
        args.append(nc.dram_tensor(f"in_{name}", a.shape, _mybir.dt.from_np(a.dtype), kind="ExternalInput").ap())
    out = nc.dram_tensor("out", (NB, S, D), _mybir.dt.float32, kind="ExternalOutput").ap()
    moe_attention_program(nc, *args, out)
    r = _run(nc, [arrays], core_ids=[0])
    return r.results[0]["out"]
```

```python
import concourse.bass as bass
from concourse import mybir
from contextlib import ExitStack

NB, S, D = 16, 512, 128
H, F, DV = 16, 16, 8
E, I = 8, 64
P = 128
NC = S // P
NT = NB * NC
GROUP = 4
NG = H // GROUP
UNITS = GROUP + 1
SLOTS = NG * UNITS
OCT = 8
NOCT = H // OCT
TILES = E * I // P + 1
HID = TILES * P
PARTS = 3
Q_SLOTS = (0, 1, 2, 0, 1, 0)
K_SLOTS = (0, 0, 0, 1, 1, 2)
KROWS = F * len(Q_SLOTS)
VW = 32
LN_EPS, TOP_EPS, ATT_EPS = 1e-5, 1e-8, 1e-9
MASKS = 2 * GROUP + 1

PAIRS, QUADS, HALVES = NB // 2, NB // 4, 2
X_GROUPS = ((0, 1), (1, 4), (4, PAIRS))
PAIR_SLOT = (None, 1, 2, 3, 8, 9, 10, 11)
LOGIT_SLOT = (2, 4, 10, 12)
FIRST_V_SLOT = 0
FIRST_PROJECT_SLOTS = (6, 7, 13, 14)
ROOT_SLOT = 5
SIGMOID_SLOT = (8, 14)
V_SLOT, PROJECT_SLOTS = 4, (11, 12, 13, 14)
SEL_SLOT = 1
DOWN_SLOT = 15

WQ, WK, WV = 0, H * F, 2 * H * F
GATE = WV + H * DV
UP = GATE + HID
WCOLS = UP + HID


def moe_attention_program(nc, x, w_in, w_v, w_o, w_down, w_route, route_bias, out):
    fp32, bf16, fp32r, i32 = mybir.dt.float32, mybir.dt.bfloat16, mybir.dt.float32r, mybir.dt.int32
    ALU, ACT, AX = mybir.AluOpType, mybir.ActivationFunctionType, mybir.AxisListType
    ctx = ExitStack()
    with ctx:
        def sb(name, shape, dt=fp32):
            return ctx.enter_context(nc.sbuf_tensor(name, shape, dt))

        def sem(name):
            return ctx.enter_context(nc.semaphore(name))

        def scratch(name, shape, dt=fp32):
            return nc.dram_tensor(name, shape, dt, kind="Internal").ap()

        sums_d = scratch("sums", [DV + 1, H, S])
        recip_d = scratch("recip", [H, S])
        sel_d = scratch("choices", [NB, E, S], bf16)

        xnT = sb("xnT", [P, NB * S])
        wts = sb("wts", [P, 2, UNITS, 1024])
        q_st = sb("q_stack", [KROWS, NOCT, OCT, S], bf16)
        k_st = sb("k_stack", [KROWS, NOCT, OCT, S], bf16)
        qk_parts = sb("qk_parts", [P, 2 * NOCT, PARTS, S], bf16)
        rest = sb("rest", [P, 2, S])
        w_hi, w_lo = sb("w_hi", [P, WCOLS], fp32r), sb("w_lo", [P, WCOLS], fp32r)
        wv_s, wo_s = sb("wv", [P, H * DV]), sb("wo", [P, D])
        wd_s = sb("wd", [P, TILES, D])
        wr_s, bias_s = sb("wr", [P, VW]), sb("route_bias_s", [P, E])
        xa_hi, xa_lo = sb("xa_hi", [P, S], fp32r), sb("xa_lo", [P, S], fp32r)
        xb_hi, xb_lo = sb("xb_hi", [P, S], fp32r), sb("xb_lo", [P, S], fp32r)
        xv = sb("xv", [P, S])
        vp = sb("v_padded", [P, NC, H, VW])
        raw = sb("raw_sums", [P, NG, S])
        w_raw = raw[:].rearrange("p g s -> p (g s)")[:, 0:WCOLS]
        num, rec, cum, att = sb("num", [P, S]), sb("rec", [P, S]), sb("cum", [P, S]), sb("att", [P, S])
        den, denr, count = sb("den", [P, S // OCT]), sb("denr", [P, S // OCT]), sb("count", [P, S // OCT])
        count_i = sb("count_i", [P, S // OCT], i32)
        ones = sb("ones", [P, S])
        sil = sb("sil", [P, 2, S])
        hid = sb("hid", [P, TILES, S])
        xres, y = sb("xres", [P, NC, D]), sb("y", [P, NC, D])
        ident = sb("ident", [P, P])
        sel = sb("sel", [P, NB, E, NC])
        selT = sb("selT", [P, QUADS, P], bf16)
        chosen = sb("chosen", [P, TILES - 1, S], bf16)
        logit = sb("logit", [P, NT, E])
        stat = sb("stat", [P, NT, 6])
        mean, var, rstd, tmp = (sb(n, [P, NT]) for n in ("mean", "var", "rstd", "tmp"))
        m1, m2, t1, sw = (sb(n, [P, NT]) for n in ("m1", "m2", "t1", "sw"))
        order = sb("order", [P, E])
        per_e, wmean = sb("per_e", [P, HALVES, 2, E]), sb("wmean", [P, 2, E])
        score, one1, one2, rt = (hid[:, n, :].rearrange("p (c e) -> p c e", e=E) for n in range(4))
        quad_logits = sil[:, 0, :]
        xn = [t[:].rearrange("p (c d) -> p c d", d=D) for t in (num, cum, rec, att)]

        ps_s = ctx.enter_context(nc.psum_tensor("ps_s", [P, 2, 1024], fp32))
        ps_av = ctx.enter_context(nc.psum_tensor("ps_av", [P, S], fp32))
        ps_x = [ctx.enter_context(nc.psum_tensor(f"ps_x{n}", [P, S], fp32)) for n in range(3)]
        (B_VT, B_G0, B_U0, B_G1, B_V, B_U1, B_G2, B_U2, B_G3, B_U3, B_G4, B_U4,
         B_Q0, B_K0, B_Q1, B_K1, B_OUT) = (ps_x[n % 3] for n in range(1, 18))
        B_G, B_U, B_P = (B_G0, B_G1, B_G2, B_G3, B_G4), (B_U0, B_U1, B_U2, B_U3, B_U4), (B_Q0, B_K0, B_Q1, B_K1)

        x_in = [sem(f"x_in{g}") for g in range(len(X_GROUPS))]
        wp_in, wp_hi, wp_split, xn_pool_step, xn_pool = (sem(n) for n in (
            "wp_in", "wp_hi", "wp_split", "xn_pool_step", "xn_pool"))
        wmean_copied, quad_ps, quad_ready = sem("wmean_copied"), sem("quad_ps"), sem("quad_ready")
        rstd_ready = sem("rstd_ready")
        w_in_sem, xt_ready, xn_ready, stats_step, rstd_step = (sem(n) for n in (
            "w_in_sem", "xt_ready", "xn_ready", "stats_step", "rstd_step"))
        biased = sem("biased")
        var_ready, sqrt_ready, xnT_ready, logits_ps, logits_ready = (sem(n) for n in (
            "var_ready", "sqrt_ready", "xnT_ready", "logits_ps", "logits_ready"))
        scores_e, route_step, per_e_ready, wmean_ps, wd_ready = (sem(n) for n in (
            "scores_e", "route_step", "per_e_ready", "wmean_ps", "wd_ready"))
        consts, const_step, w_split, w_split_hi, sel_ready = (sem(n) for n in (
            "consts", "const_step", "w_split", "w_split_hi", "sel_ready"))
        table_ready = sem("table_ready")
        turns = sem("turns")
        scores_ready = sem("scores_ready")
        squares_ready = sem("squares_ready")
        masked = sem("masked")
        av_ready = sem("av_ready")
        raw_ready = sem("raw_ready")
        selT_ps, selT_ready, sel_out, chosen_in, hid_masked = (sem(n) for n in (
            "selT_ps", "selT_ready", "sel_out", "chosen_in", "hid_masked"))
        vt_ps, cum_ready = sem("vt_ps"), sem("cum_ready")
        gate_ps, up_ps, silu_ready, hid_ready = sem("gate_ps"), sem("up_ps"), sem("silu_ready"), sem("hid_ready")
        v_ps, vp_ready = sem("v_ps"), sem("vp_ready")
        qk_ps, part0_ready, rest_ready, part1_ready, part2_ready = (sem(n) for n in (
            "qk_ps", "part0_ready", "rest_ready", "part1_ready", "part2_ready"))
        xb_hi_ready, xb_ready, xa_hi_ready, xa_ready, xv_ready = (sem(n) for n in (
            "xb_hi_ready", "xb_ready", "xa_hi_ready", "xa_ready", "xv_ready"))
        den_sum, recip_ready, num_sum, att_ready, out_ps, y_ready = (sem(n) for n in (
            "den_sum", "recip_ready", "num_sum", "att_ready", "out_ps", "y_ready"))
        stack_in = [sem(f"stack_in{o}") for o in range(NOCT)]
        STACK_DMAS = 2 * len(Q_SLOTS)
        xres_in, sums_out, num_in, den_in, recip_out, rec_in, y_out = (sem(n) for n in (
            "xres_in", "sums_out", "num_in", "den_in", "recip_out", "rec_in", "y_out"))

        block = ctx.enter_context(nc.Block())

        def batch_cols(b):
            return bass.ds(b * S, S) if not isinstance(b, int) else slice(b * S, b * S + S)

        def tile_bank(b, t):
            if isinstance(b, int) and b == 0:
                return ps_s[:, t // 2, (t % 2) * S:(t % 2 + 1) * S]
            return B_P[t][:]

        def group_of(k):
            return next(g for g, (k0, k1) in enumerate(X_GROUPS) if k0 <= k < k1)

        def rows_of(t, b):
            return t[bass.ds(b, 1)].rearrange("a (c p) d -> p (a c) d", p=P)

        @block.sync
        def _(sp):
            def x_load(g):
                k0, k1 = X_GROUPS[g]
                sp.dma_start(xnT[:, 2 * k0 * S:2 * k1 * S].rearrange("p (k d) -> p k d", d=D),
                             x[2 * k0:2 * k1].rearrange("b (c p) d -> p (b c) d", p=P)).then_inc(x_in[g], 16)

            x_load(0)
            sp.dma_start(w_raw[:, 0:GATE], w_in[:, 0:GATE]).then_inc(wp_in, 16)
            x_load(1)
            for dst, src in ((wr_s[:, 0:E], w_route), (bias_s[:], route_bias.partition_broadcast(P)),
                             (w_raw[:, GATE:WCOLS], w_in[:, GATE:WCOLS]), (wv_s[:], w_v), (wo_s[:], w_o),
                             (wd_s[:], w_down)):
                sp.dma_start(dst, src).then_inc(w_in_sem, 16)

            def stacks(b, o):
                if not isinstance(b, int) or b > 0:
                    sp.wait_ge(scores_ready, (b - 1) * SLOTS + 2 * UNITS * (o + 1))
                    sp.sem_inc(turns, 1)
                for n, (stack, slots) in enumerate(((q_st, Q_SLOTS), (k_st, K_SLOTS))):
                    tile = 2 * o + n
                    for part, ready in enumerate((part0_ready, part1_ready, part2_ready)):
                        sp.wait_ge(ready, b * 4 + tile + 1)
                        sp.sem_inc(turns, 1)
                        for r in range(len(slots)):
                            if slots[r] == part:
                                sp.dma_start(stack[r * F:(r + 1) * F, o], qk_parts[:, tile, part]).then_inc(stack_in[o], 16)

            def load_chosen(b):
                for half in range(2):
                    src = sel_d[bass.ds(b, 1)].rearrange("a (j t) s -> t a j s", t=2)[half]
                    sp.dma_start(chosen[half * I:(half + 1) * I],
                                 src.to_broadcast([I, TILES - 1, S])).then_inc(chosen_in, 16)

            def iteration(i, attend, experts, project):
                f, n = i - 1, i + 1
                if attend:
                    stacks(i, 1)
                if experts:
                    if not isinstance(f, int) or f > 0:
                        sp.wait_ge(y_ready, f)
                        sp.sem_inc(turns, 1)
                    sp.dma_start(xres[:], rows_of(x, f)).then_inc(xres_in, 16)
                    if isinstance(i, int) and i == 1:
                        sp.wait_ge(selT_ready, 1)
                        sp.dma_start(sel_d.rearrange("(q b) e (c p) -> (b e c) q p", b=4, p=P), selT[:]).then_inc(sel_out, 16)
                        sp.wait_ge(sel_out, 16)
                        load_chosen(0)
                    sp.wait_ge(raw_ready, f * NG + NG)
                    for j in range(GROUP):
                        sp.dma_start(sums_d[:, j * NG:(j + 1) * NG, :],
                                     raw[32 * j:32 * j + DV + 1]).then_inc(sums_out, 16)
                    sp.wait_ge(sums_out, f * (16 * GROUP) + 16 * GROUP)
                    sp.dma_start(den[:], sums_d[DV].rearrange("h (k s) -> (h k) s", s=S // OCT)).then_inc(den_in, 16)
                    if not isinstance(f, int) or f > 0:
                        sp.wait_ge(num_sum, f)
                    sp.dma_start(num[:], sums_d[0:DV].rearrange("d h s -> h d s")).then_inc(num_in, 16)
                    sp.wait_ge(recip_ready, f + 1)
                    sp.dma_start(recip_d.rearrange("h (k s) -> (h k) s", s=S // OCT), denr[:]).then_inc(recip_out, 16)
                    sp.wait_ge(recip_out, f * 16 + 16)
                    if not isinstance(f, int) or f > 0:
                        sp.wait_ge(att_ready, f)
                    sp.dma_start(rec[:], recip_d.unsqueeze(1).to_broadcast([H, DV, S])).then_inc(rec_in, 16)
                if attend and experts:
                    sp.wait_ge(hid_masked, f * (TILES - 1) + TILES - 1)
                    sp.sem_inc(turns, 1)
                    load_chosen(i)
                if project:
                    stacks(n, 0)
                if experts:
                    sp.wait_ge(y_ready, f + 1)
                    sp.sem_inc(turns, 1)
                    sp.dma_start(rows_of(out, f), y[:]).then_inc(y_out, 16)

            stacks(0, 0)
            x_load(2)
            iteration(0, True, False, True)
            iteration(1, True, True, True)
            with sp.Fori(2, NB - 1) as i:
                iteration(i, True, True, True)
            iteration(NB - 1, True, True, False)
            iteration(NB, False, True, False)
            sp.wait_ge(y_out, 16 * NB)

        @block.gpsimd
        def _(pool):
            nc.gpsimd.memset(wr_s[:, E:VW], 0.0).then_inc(const_step, 1)
            nc.gpsimd.memset(ident[:], 0.0).then_inc(const_step, 1)
            nc.gpsimd.memset(vp[:], 0.0).then_inc(const_step, 1)
            nc.gpsimd.memset(ones[:], 1.0).then_inc(const_step, 1)
            pool.wait_ge(const_step, 4)
            nc.gpsimd.affine_select(out=ident[:], in_=ident[:], compare_op=ALU.not_equal, fill=1.0, base=0,
                                    pattern=[[-1, P]], channel_multiplier=1).then_inc(consts, 1)
            nc.gpsimd.memset(vp[:, :, :, DV:DV + 1], 1.0).then_inc(consts, 1)
            nc.gpsimd.iota(order[:], pattern=[[-1, E]], base=E, channel_multiplier=0,
                           allow_small_or_imprecise_dtypes=True).then_inc(consts, 1)
            nc.gpsimd.iota(count_i[:], pattern=[[1, S // OCT]], base=0, channel_multiplier=S // OCT).then_inc(consts, 1)

            def mask(b, u):
                g, j = divmod(u, UNITS)
                w = wts[:, g % 2, j, :]
                pool.wait_ge(squares_ready, b * SLOTS + u + 1)
                pool.sem_inc(turns, 1)
                keep = dict(compare_op=ALU.is_ge, fill=0.0, base=0, channel_multiplier=-1)
                if j < GROUP:
                    v = w.rearrange("p (a n) -> p a n", a=2)[:, :, 0:P]
                    nc.gpsimd.affine_select(out=v, in_=v, pattern=[[0, 2], [1, P]], **keep).then_inc(masked, 1)
                    v = w[:, 1024 - P:1024]
                    nc.gpsimd.affine_select(out=v, in_=v, pattern=[[1, P]], **keep).then_inc(masked, 1)
                else:
                    v = w.rearrange("p (a n) -> p a n", a=GROUP)[:, :, 0:P]
                    nc.gpsimd.affine_select(out=v, in_=v, pattern=[[0, GROUP], [1, P]], **keep).then_inc(masked, 1)

            def normalise(k):
                pool.wait_ge(rstd_ready, group_of(k) + 1)
                if k >= 2:
                    pool.wait_ge(xt_ready, 2 * (k - 1))
                for b in (2 * k, 2 * k + 1):
                    row = b * NC + NC - 1
                    to = xn[b % 4][:, NC - 1, :]
                    nc.gpsimd.tensor_tensor(to, xnT[:, row * D:row * D + D], mean[:, row:row + 1].to_broadcast([P, D]),
                                            ALU.subtract).then_inc(xn_pool_step, 1)
                    pool.wait_ge(xn_pool_step, b + 1)
                    nc.gpsimd.tensor_tensor(to, to, rstd[:, row:row + 1].to_broadcast([P, D]),
                                            ALU.mult).then_inc(xn_pool, 1)

            normalise(0)

            def split_x(b, hi, lo, hi_sem, lo_sem, count):
                pool.wait_ge(xnT_ready, b + 1)
                nc.gpsimd.tensor_copy(hi[:], xnT[:, batch_cols(b)]).then_inc(hi_sem, 1)
                pool.wait_ge(hi_sem, count)
                nc.gpsimd.tensor_tensor(lo[:], xnT[:, batch_cols(b)], hi[:].bitcast(fp32),
                                        ALU.subtract).then_inc(lo_sem, 1)

            split_x(0, xa_hi, xa_lo, xa_hi_ready, xa_ready, 1)
            pool.wait_ge(w_in_sem, 16 * 6)
            cols = slice(GATE, WCOLS)
            nc.gpsimd.tensor_copy(w_hi[:, cols], w_raw[:, cols]).then_inc(w_split_hi, 1)
            pool.wait_ge(w_split_hi, 1)
            nc.gpsimd.tensor_tensor(w_lo[:, cols], w_raw[:, cols], w_hi[:, cols].bitcast(fp32),
                                    ALU.subtract).then_inc(w_split, 1)
            pool.wait_ge(qk_ps, 4)
            split_x(1, xb_hi, xb_lo, xb_hi_ready, xb_ready, 2)

            def iteration(i):
                for u in range(SLOTS):
                    mask(i, u)

            for u in range(-2, SLOTS):
                if u >= 0:
                    mask(0, u)
                if u + 2 in PAIR_SLOT:
                    normalise(PAIR_SLOT.index(u + 2))
            with pool.Fori(1, NB) as i:
                iteration(i)

        @block.scalar
        def _(act):
            def root(g):
                rows = slice(2 * NC * X_GROUPS[g][0], 2 * NC * X_GROUPS[g][1])
                act.wait_ge(var_ready, g + 1)
                nc.scalar.activation(tmp[:, rows], var[:, rows], ACT.Sqrt).then_inc(sqrt_ready, 1)

            def transposed(k):
                for b in (2 * k, 2 * k + 1):
                    act.wait_ge(xt_ready, b + 1)
                    nc.scalar.activation(xnT[:, batch_cols(b)], ps_x[b % 2][:], ACT.Copy).then_inc(xnT_ready, 1)

            def quad_out(q):
                act.wait_ge(quad_ps, q + 1)
                nc.scalar.activation(quad_logits, ps_x[2][:], ACT.Copy).then_inc(quad_ready, 1)

            def logits_out(q):
                act.wait_ge(logits_ps, q + 1)
                nc.scalar.activation(
                    logit[:, 4 * q * NC:4 * (q + 1) * NC, :].rearrange("p (b c) e -> p c b e", c=NC),
                    ps_x[2][:].rearrange("p (c b w) -> p c b w", b=4, w=VW)[:, :, :, 0:E], ACT.Copy).then_inc(logits_ready, 1)

            def sigmoids(h):
                rows = slice(h * NT // HALVES, (h + 1) * NT // HALVES)
                act.wait_ge(biased, h + 1)
                nc.scalar.activation(score[:, rows, :], logit[:, rows, :], ACT.Sigmoid).then_inc(scores_e, 1)

            def square(b, u):
                g, j = divmod(u, UNITS)
                act.wait_ge(scores_ready, b * SLOTS + u + 1)
                if j == 0 and not (isinstance(b, int) and b == 0 and g < 2):
                    act.wait_ge(av_ready, b * NG + g - 1)
                nc.scalar.activation(wts[:, g % 2, j, :], ps_s[:, u % 2, :], ACT.Square, bias=1.0,
                                     scale=0.25).then_inc(squares_ready, 1)

            def sums_out_of_psum(b, g):
                act.wait_ge(av_ready, b * NG + g + 1)
                if g == 0 and not (isinstance(b, int) and b == 0):
                    act.wait_ge(sums_out, b * (16 * GROUP))
                nc.scalar.activation(raw[:, g, :], ps_av[:], ACT.Copy).then_inc(raw_ready, 1)

            def silu(b, j):
                act.wait_ge(gate_ps, b * TILES + j + 1)
                if j >= 2:
                    act.wait_ge(hid_ready, b * TILES + j - 1)
                elif not (isinstance(b, int) and b == 0):
                    act.wait_ge(hid_ready, b * TILES)
                elif j == 0:
                    act.wait_ge(table_ready, 1)
                nc.scalar.activation(sil[:, j % 2, :], B_G[j][:], ACT.Silu).then_inc(silu_ready, 1)

            def part0(b, t):
                act.wait_ge(qk_ps, b * 4 + t + 1)
                if not (isinstance(b, int) and b == 0):
                    act.wait_ge(stack_in[t // 2], b * (16 * STACK_DMAS))
                nc.scalar.activation(qk_parts[:, t, 0, :], tile_bank(b, t), ACT.Copy).then_inc(part0_ready, 1)

            def part1(b, t):
                act.wait_ge(rest_ready, b * 4 + t + 1)
                nc.scalar.activation(qk_parts[:, t, 1, :], rest[:, t % 2, :], ACT.Copy).then_inc(part1_ready, 1)

            def v_out(b):
                act.wait_ge(v_ps, b + 1)
                if not (isinstance(b, int) and b == 0):
                    act.wait_ge(av_ready, b * NG)
                else:
                    act.wait_ge(consts, 4)
                nc.scalar.activation(vp[:].rearrange("p c h w -> p (c h) w")[:, :, 0:DV],
                                     B_V[:].rearrange("p (k d) -> p k d", d=DV), ACT.Copy).then_inc(vp_ready, 1)

            def iteration(i, attend, experts, project):
                f, n = i - 1, i + 1
                first, final = (isinstance(i, int) and i == k for k in (0, NB))
                if final:
                    sums_out_of_psum(f, NG - 1)
                project_slots = FIRST_PROJECT_SLOTS if first else PROJECT_SLOTS
                for u in range(SLOTS):
                    if attend:
                        square(i, u)
                    if first:
                        for q, slot in enumerate(LOGIT_SLOT):
                            if u == slot:
                                quad_out(q)
                            if u == slot + 1:
                                logits_out(q)
                        if u in PAIR_SLOT:
                            transposed(PAIR_SLOT.index(u))
                        if u in SIGMOID_SLOT:
                            sigmoids(SIGMOID_SLOT.index(u))
                    if u == SEL_SLOT and isinstance(i, int) and i == 1:
                        act.wait_ge(selT_ps, 1)
                        nc.scalar.activation(selT[:].rearrange("p q n -> p (q n)"), ps_x[0][:],
                                             ACT.Copy).then_inc(selT_ready, 1)
                    if experts and u in (1, 3, 5, 7, 9):
                        silu(f, (u - 1) // 2)
                    if u == 4 and experts and not final:
                        sums_out_of_psum(f, NG - 1)
                    if u == (FIRST_V_SLOT if first else V_SLOT) and attend:
                        v_out(i)
                    if first and u == ROOT_SLOT:
                        root(2)
                    if attend and u in (9, 14, 19):
                        if first and u == 9:
                            act.wait_ge(w_split, 1)
                        sums_out_of_psum(i, u // UNITS - 1)
                    if project and u in project_slots:
                        part0(n, project_slots.index(u))

            root(0)
            transposed(0)
            for t in range(4):
                part0(0, t)
                if t > 0:
                    part1(0, t - 1)
            part1(0, 3)
            root(1)
            iteration(0, True, False, True)
            act.wait_ge(logits_ps, QUADS)
            nc.scalar.activation(sil[:, 0, 0:1], ones[:, 0:1], ACT.Silu).then_inc(table_ready, 1)
            iteration(1, True, True, True)
            with act.Fori(2, NB - 1) as i:
                iteration(i, True, True, True)
            iteration(NB - 1, True, True, False)
            iteration(NB, False, True, False)

        @block.vector
        def _(dve):
            steps = {}

            def step(ins, s):
                steps[s.name] = steps.get(s.name, 0) + 1
                ins.then_inc(s, 1)
                dve.wait_ge(s, steps[s.name])

            def split_weights(cols, hi_sem, lo_sem):
                nc.vector.tensor_copy(w_hi[:, cols], w_raw[:, cols]).then_inc(hi_sem, 1)
                dve.wait_ge(hi_sem, 1)
                nc.vector.tensor_tensor(w_lo[:, cols], w_raw[:, cols], w_hi[:, cols].bitcast(fp32),
                                        ALU.subtract).then_inc(lo_sem, 1)

            def statistics(k):
                for c in range(k * 2 * NC, (k + 1) * 2 * NC):
                    nc.vector.bn_stats(stat[:, c, :], xnT[:, c * D:(c + 1) * D]).then_inc(stats_step, 1)

            def mean_and_rstd(g):
                r = slice(2 * NC * X_GROUPS[g][0], 2 * NC * X_GROUPS[g][1])
                dve.wait_ge(stats_step, r.stop)
                nc.vector.tensor_tensor(m1[:, r], stat[:, r, 1], stat[:, r, 4], ALU.subtract).then_inc(rstd_step, 1)
                nc.vector.tensor_tensor(m2[:, r], stat[:, r, 2], stat[:, r, 5], ALU.add).then_inc(rstd_step, 1)
                nc.vector.tensor_tensor(mean[:, r], stat[:, r, 1], stat[:, r, 4], ALU.add).then_inc(rstd_step, 1)
                steps[rstd_step.name] = steps.get(rstd_step.name, 0) + 3
                dve.wait_ge(rstd_step, steps[rstd_step.name])
                step(nc.vector.scalar_tensor_tensor(m1[:, r], m1[:, r], 0.25, m1[:, r], ALU.mult, ALU.mult), rstd_step)
                step(nc.vector.scalar_tensor_tensor(var[:, r], m2[:, r], 1.0 / D, m1[:, r], ALU.mult, ALU.add), rstd_step)
                nc.vector.tensor_scalar(var[:, r], var[:, r], LN_EPS, None, ALU.add).then_inc(var_ready, 1)
                step(nc.vector.tensor_scalar(mean[:, r], mean[:, r], 0.5, None, ALU.mult), rstd_step)
                dve.wait_ge(sqrt_ready, g + 1)
                step(nc.vector.reciprocal(rstd[:, r], tmp[:, r]), rstd_step)
                step(nc.vector.tensor_tensor(t1[:, r], rstd[:, r], rstd[:, r], ALU.mult), rstd_step)
                step(nc.vector.scalar_tensor_tensor(t1[:, r], t1[:, r], -0.5, var[:, r], ALU.mult, ALU.mult), rstd_step)
                nc.vector.scalar_tensor_tensor(rstd[:, r], t1[:, r], 1.5, rstd[:, r], ALU.add,
                                               ALU.mult).then_inc(rstd_ready, 1)
                dve.wait_ge(rstd_ready, g + 1)

            def normalise(k):
                if k >= 2:
                    dve.wait_ge(xt_ready, 2 * (k - 1))
                for b in (2 * k, 2 * k + 1):
                    for c in range(NC - 1):
                        row = b * NC + c
                        nc.vector.tensor_scalar(xn[b % 4][:, c, :], xnT[:, row * D:row * D + D], mean[:, row:row + 1],
                                                rstd[:, row:row + 1], ALU.subtract, ALU.mult).then_inc(xn_ready, 1)

            def split_x(b, hi, lo, hi_sem, lo_sem):
                nc.vector.tensor_scalar(hi[:], xnT[:, batch_cols(b)], 1.0, None, ALU.mult).then_inc(hi_sem, 1)
                dve.wait_ge(hi_sem, b + 1)
                nc.vector.tensor_tensor(lo[:], xnT[:, batch_cols(b)], hi[:].bitcast(fp32),
                                        ALU.subtract).then_inc(lo_sem, 1)

            def tile_rest(b, t):
                dve.wait_ge(part0_ready, b * 4 + t + 1)
                if t >= 2 or not (isinstance(b, int) and b == 0):
                    dve.wait_ge(part2_ready, b * 4 + t - 1)
                nc.vector.tensor_tensor(rest[:, t % 2, :], tile_bank(b, t), qk_parts[:, t, 0, :],
                                        ALU.subtract).then_inc(rest_ready, 1)

            def part2(b, t):
                dve.wait_ge(part1_ready, b * 4 + t + 1)
                nc.vector.tensor_tensor(qk_parts[:, t, 2, :], rest[:, t % 2, :], qk_parts[:, t, 1, :],
                                        ALU.subtract).then_inc(part2_ready, 1)

            def split_tile(b, t):
                tile_rest(b, t)
                dve.wait_ge(rest_ready, b * 4 + t + 1)
                nc.vector.tensor_copy(qk_parts[:, t, 1, :], rest[:, t % 2, :]).then_inc(part1_ready, 1)
                part2(b, t)

            def hidden(b, j):
                dve.wait_ge(up_ps, b * TILES + j + 1)
                dve.wait_ge(silu_ready, b * TILES + j + 1)
                if j == 0 and not (isinstance(b, int) and b == 0):
                    dve.wait_ge(out_ps, b)
                nc.vector.tensor_tensor(hid[:, j, :], B_U[j][:], sil[:, j % 2, :], ALU.mult).then_inc(hid_ready, 1)

            def mask_hidden(b, j):
                if j == 0:
                    dve.wait_ge(chosen_in, b * 32 + 32)
                dve.wait_ge(hid_ready, b * TILES + j + 1)
                nc.vector.tensor_tensor(hid[:, j, :], hid[:, j, :], chosen[:, j, :], ALU.mult).then_inc(hid_masked, 1)

            def copy_xv(b):
                if not isinstance(b, int) or b > 0:
                    dve.wait_ge(v_ps, b)
                nc.vector.tensor_scalar(xv[:], xnT[:, batch_cols(b)], 1.0, None, ALU.mult).then_inc(xv_ready, 1)

            def add_route_bias(h):
                dve.wait_ge(logits_ready, (h + 1) * QUADS // HALVES)
                rows = slice(h * NT // HALVES, (h + 1) * NT // HALVES)
                nc.vector.tensor_tensor(logit[:, rows, :], logit[:, rows, :],
                                        bias_s[:].unsqueeze(1).to_broadcast([P, NT // HALVES, E]),
                                        ALU.add).then_inc(biased, 1)

            def routing(h):
                dve.wait_ge(scores_e, h + 1)
                dve.wait_ge(consts, 4)
                rows = slice(h * NT // HALVES, (h + 1) * NT // HALVES)
                wide = [P, NT // HALVES, E]
                o = order[:].unsqueeze(1).to_broadcast(wide)
                sc, first_one, second_one, r = (t[:, rows, :] for t in (score, one1, one2, rt))
                best1, best2, top = (t[:, rows] for t in (m1, m2, t1))

                def b3(t):
                    return t.unsqueeze(2).to_broadcast(wide)

                def best(m, one):
                    step(nc.vector.tensor_reduce(m, sc, AX.X, ALU.max), route_step)
                    step(nc.vector.tensor_tensor(r, sc, b3(m), ALU.is_equal), route_step)
                    step(nc.vector.tensor_tensor(r, r, o, ALU.mult), route_step)
                    step(nc.vector.tensor_reduce(top, r, AX.X, ALU.max), route_step)
                    step(nc.vector.tensor_tensor(one, r, b3(top), ALU.is_equal), route_step)

                best(best1, first_one)
                step(nc.vector.scalar_tensor_tensor(sc, first_one, -4.0, sc, ALU.mult, ALU.add), route_step)
                best(best2, second_one)
                step(nc.vector.tensor_tensor(r, first_one, second_one, ALU.add), route_step)
                nc.vector.tensor_scalar(
                    sel[:, h * NB // HALVES:(h + 1) * NB // HALVES].rearrange("p b e c -> p b c e"),
                    r.rearrange("p (b c) e -> p b c e", c=NC), 1.0, None, ALU.mult).then_inc(sel_ready, 1)

            def route_weights(h):
                rows = slice(h * NT // HALVES, (h + 1) * NT // HALVES)
                first_one, second_one, r = (t[:, rows, :] for t in (one1, one2, rt))
                best1, best2, total = (t[:, rows] for t in (m1, m2, sw))

                def b3(t):
                    return t.unsqueeze(2).to_broadcast([P, NT // HALVES, E])

                step(nc.vector.tensor_reduce(per_e[:, h, 1, :], r.rearrange("p c e -> p e c"), AX.X, ALU.add), route_step)
                step(nc.vector.scalar_tensor_tensor(total, best1, TOP_EPS, best2, ALU.add, ALU.add), route_step)
                step(nc.vector.reciprocal(total, total), route_step)
                step(nc.vector.tensor_tensor(best1, best1, total, ALU.mult), route_step)
                step(nc.vector.tensor_tensor(best2, best2, total, ALU.mult), route_step)
                step(nc.vector.tensor_tensor(first_one, first_one, b3(best1), ALU.mult), route_step)
                step(nc.vector.tensor_tensor(second_one, second_one, b3(best2), ALU.mult), route_step)
                step(nc.vector.tensor_tensor(r, first_one, second_one, ALU.add), route_step)
                nc.vector.tensor_reduce(per_e[:, h, 0, :], r.rearrange("p c e -> p e c"), AX.X,
                                        ALU.add).then_inc(per_e_ready, 1)

            def mean_weights():
                dve.wait_ge(wmean_ps, 1)
                nc.vector.tensor_copy(wmean[:], B_Q1[:, 0:2 * E].rearrange("p (a e) -> p a e", a=2)).then_inc(wmean_copied, 1)
                dve.wait_ge(wmean_copied, 1)
                step(nc.vector.tensor_scalar(wmean[:, 1, :], wmean[:, 1, :], 1.0, None, ALU.max), route_step)
                step(nc.vector.reciprocal(wmean[:, 1, :], wmean[:, 1, :]), route_step)
                step(nc.vector.tensor_tensor(wmean[:, 0, :], wmean[:, 0, :], wmean[:, 1, :], ALU.mult), route_step)

            def weigh_down():
                dve.wait_ge(w_in_sem, 16 * 6)
                for e in range(E):
                    r = slice(I * (e % 2), I * (e % 2) + I)
                    nc.vector.tensor_scalar(wd_s[r, e // 2, :], wd_s[r, e // 2, :], wmean[r, 0, e:e + 1], None,
                                            ALU.mult).then_inc(wd_ready, 1)

            def token_counts():
                dve.wait_ge(consts, 4)
                step(nc.vector.tensor_single_scalar(count_i[:], count_i[:], S - 1, ALU.bitwise_and), route_step)
                step(nc.vector.tensor_copy(count[:], count_i[:]), route_step)
                step(nc.vector.tensor_scalar(count[:], count[:], 1.0, None, ALU.add), route_step)

            def prepare_group(g):
                dve.wait_ge(x_in[g], 16)
                for k in range(*X_GROUPS[g]):
                    if k > 1:
                        statistics(k)
                mean_and_rstd(g)
                for k in range(*X_GROUPS[g]):
                    normalise(k)
                    if k == X_GROUPS[2][0]:
                        add_route_bias(0)
                    if g == 2 and k - X_GROUPS[2][0] < 2:
                        split_tile(1, k - X_GROUPS[2][0])

            def iteration(i, attend, experts, project):
                f, n = i - 1, i + 1
                second = isinstance(i, int) and i == 1
                if project and experts:
                    dve.wait_ge(qk_ps, n * 4)
                    split_x(n, xb_hi, xb_lo, xb_hi_ready, xb_ready)
                if experts:
                    dve.wait_ge(vt_ps, f + 1)
                    nc.vector.tensor_tensor_scan(cum[:], ones[:], B_VT[:], 0.0, ALU.mult, ALU.add).then_inc(cum_ready, 1)
                    for j in range(TILES - 1):
                        if second and j < HALVES:
                            route_weights(j)
                        hidden(f, j)
                        if j > 0:
                            mask_hidden(f, j - 1)
                    dve.wait_ge(den_in, f * 16 + 16)
                    if not isinstance(f, int) or f > 0:
                        dve.wait_ge(recip_out, f * 16)
                    nc.vector.scalar_tensor_tensor(den[:], den[:], 2 * ATT_EPS, count[:], ALU.add,
                                                   ALU.add).then_inc(den_sum, 1)
                    dve.wait_ge(den_sum, f + 1)
                    nc.vector.reciprocal(denr[:], den[:]).then_inc(recip_ready, 1)
                    hidden(f, TILES - 1)
                    mask_hidden(f, TILES - 2)
                if attend and experts:
                    dve.wait_ge(up_ps, f * TILES + TILES)
                    split_x(i, xa_hi, xa_lo, xa_hi_ready, xa_ready)
                if not experts:
                    prepare_group(2)
                    routing(0)
                    add_route_bias(1)
                    split_tile(1, 2)
                    split_tile(1, 3)
                    routing(1)
                if project and experts:
                    split_tile(n, 0)
                    if second:
                        mean_weights()
                        weigh_down()
                    split_tile(n, 1)
                if experts:
                    dve.wait_ge(num_in, f * 16 + 16)
                    dve.wait_ge(cum_ready, f + 1)
                    nc.vector.tensor_tensor(cum[:], num[:], cum[:], ALU.add).then_inc(num_sum, 1)
                    dve.wait_ge(num_sum, f + 1)
                    dve.wait_ge(rec_in, f * 16 + 16)
                    if not isinstance(f, int) or f > 0:
                        dve.wait_ge(out_ps, f)
                    nc.vector.tensor_tensor(att[:], cum[:], rec[:], ALU.mult).then_inc(att_ready, 1)
                if project:
                    if experts:
                        split_tile(n, 2)
                        split_tile(n, 3)
                    copy_xv(n)
                if experts:
                    dve.wait_ge(out_ps, f + 1)
                    dve.wait_ge(xres_in, f * 16 + 16)
                    if not isinstance(f, int) or f > 0:
                        dve.wait_ge(y_out, f * 16)
                    nc.vector.tensor_tensor(y[:], B_OUT[:].rearrange("p (c d) -> p c d", d=D), xres[:],
                                            ALU.add).then_inc(y_ready, 1)

            dve.wait_ge(x_in[0], 16)
            statistics(0)
            mean_and_rstd(0)
            normalise(0)
            dve.wait_ge(wp_in, 16)
            split_weights(slice(0, GATE), wp_hi, wp_split)
            dve.wait_ge(xnT_ready, 1)
            split_x(0, xb_hi, xb_lo, xb_hi_ready, xb_ready)
            copy_xv(0)
            token_counts()
            dve.wait_ge(x_in[1], 16)
            statistics(1)
            for t in range(4):
                tile_rest(0, t)
                if t > 0:
                    part2(0, t - 1)
            part2(0, 3)
            prepare_group(1)
            iteration(0, True, False, True)
            iteration(1, True, True, True)
            with dve.Fori(2, NB - 1) as i:
                iteration(i, True, True, True)
            iteration(NB - 1, True, True, False)
            iteration(NB, False, True, False)

        @block.tensor
        def _(pe):
            pe.wait_ge(consts, 4)

            def transpose_pair(k):
                if k >= 1:
                    pe.wait_ge(xnT_ready, 2 * k)
                for b in (2 * k, 2 * k + 1):
                    pe.wait_ge(xn_ready, (b + 1) * (NC - 1))
                    pe.wait_ge(xn_pool, b + 1)
                    for c in range(NC):
                        last = nc.tensor.transpose(ps_x[b % 2][:, c * P:(c + 1) * P], xn[b % 4][:, c, :], ident[:])
                    last.then_inc(xt_ready, 1)

            def routing_logits(q):
                pe.wait_ge(xnT_ready, 4 * q + 4)
                if q == 0:
                    pe.wait_ge(w_in_sem, 16 * 6)
                else:
                    pe.wait_ge(logits_ready, q)
                for j in range(4):
                    last = nc.tensor.matmul(ps_x[2][32 * j:32 * j + VW, :], wr_s[:], xnT[:, batch_cols(4 * q + j)],
                                            start=True, stop=True)
                last.then_inc(quad_ps, 1)

            def transpose_logits(q):
                pe.wait_ge(quad_ready, q + 1)
                for c in range(NC):
                    last = nc.tensor.transpose(ps_x[2][:, c * P:(c + 1) * P], quad_logits[:, c * P:(c + 1) * P], ident[:])
                last.then_inc(logits_ps, 1)

            def three(bank, col, hi, lo):
                nc.tensor.matmul(bank, w_hi[:, col:col + P], hi[:], start=True, stop=False)
                nc.tensor.matmul(bank, w_lo[:, col:col + P], hi[:], start=False, stop=False)
                return nc.tensor.matmul(bank, w_hi[:, col:col + P], lo[:], start=False, stop=True)

            def project_tile(b, t):
                o, n = divmod(t, 2)
                col = (WQ, WK)[n] + o * P
                three(tile_bank(b, t), col, xb_hi, xb_lo).then_inc(qk_ps, 1)

            def scores(b, u):
                g, j = divmod(u, UNITS)
                o = g // 2
                if not (isinstance(b, int) and b == 0 and u < 2):
                    pe.wait_ge(squares_ready, b * SLOTS + u - 1)
                if u % (2 * UNITS) == 0:
                    pe.wait_ge(stack_in[o], b * (16 * STACK_DMAS) + 16 * STACK_DMAS)

                def chunk(head, key, dst):
                    h = head % OCT
                    return nc.tensor.matmul(dst, k_st[:, o, h, key * P:(key + 1) * P],
                                            q_st[:, o, h, key * P:S], start=True, stop=True)
                ps = ps_s[:, u % 2, :]
                if j < GROUP:
                    chunk(g * GROUP + j, 3, ps[:, 896:1024])
                    chunk(g * GROUP + j, 1, ps[:, 512:896])
                    last = chunk(g * GROUP + j, 0, ps[:, 0:512])
                else:
                    for jj in range(GROUP):
                        last = chunk(g * GROUP + jj, 2, ps[:, jj * 256:(jj + 1) * 256])
                last.then_inc(scores_ready, 1)

            AV = ((0, 0, 512), (1, 512, 896), (3, 896, 1024), (2, None, None))

            def weighted(b, g, n):
                key, lo, hi = AV[n]
                if n == 0:
                    pe.wait_ge(masked, b * (NG * MASKS) + (g + 1) * MASKS)
                    if not (isinstance(b, int) and b == 0 and g == 0):
                        pe.wait_ge(raw_ready, b * NG + g)
                    if g == 0:
                        pe.wait_ge(vp_ready, b + 1)
                for j in range(GROUP):
                    w = wts[:, g % 2, j, lo:hi] if key != 2 else wts[:, g % 2, GROUP, j * 256:(j + 1) * 256]
                    last = nc.tensor.matmul(ps_av[32 * j:32 * j + VW, key * P:S], vp[:, key, g * GROUP + j, :], w,
                                            start=(n == 0), stop=(n == 3))
                if n == 3:
                    last.then_inc(av_ready, 1)

            def gate(b, j):
                three(B_G[j][:], GATE + j * P, xa_hi, xa_lo).then_inc(gate_ps, 1)

            def up(b, j):
                three(B_U[j][:], UP + j * P, xa_hi, xa_lo).then_inc(up_ps, 1)

            def down(b, c, j):
                tok = slice(c * P, (c + 1) * P)
                nc.tensor.matmul(B_OUT[:, tok], hid[:, j, tok], wd_s[:, j, :], start=(c == 0 and j == 0),
                                 stop=False, skip_group_check=True)

            def attention_out(b):
                pe.wait_ge(att_ready, b + 1)
                for c in range(NC):
                    tok = slice(c * P, (c + 1) * P)
                    last = nc.tensor.matmul(B_OUT[:, tok], att[:, tok], wo_s[:], start=False, stop=(c == NC - 1),
                                            skip_group_check=True)
                last.then_inc(out_ps, 1)

            def iteration(i, attend, experts, project):
                f, n = i - 1, i + 1
                first, second, final = (isinstance(i, int) and i == k for k in (0, 1, NB))
                project_slots = FIRST_PROJECT_SLOTS if first else PROJECT_SLOTS
                if final:
                    for j in range(GROUP):
                        weighted(f, NG - 1, j)
                for u in range(SLOTS):
                    g, j = divmod(u, UNITS)
                    if attend:
                        scores(i, u)
                    if experts:
                        if u == 0:
                            pe.wait_ge(xa_ready, f + 1)
                            if not final:
                                pe.wait_ge(rest_ready, i * 4 + 4)
                            three(B_VT[:], WV, xa_hi, xa_lo).then_inc(vt_ps, 1)
                        if u == 1:
                            pe.wait_ge(y_ready, f)
                            gate(f, 0)
                        if u == 2:
                            if final:
                                pe.wait_ge(hid_ready, f * TILES)
                            else:
                                pe.wait_ge(rest_ready, i * 4 + 3)
                            if second:
                                pe.wait_ge(selT_ready, 1)
                            up(f, 0)
                        if u == 3:
                            pe.wait_ge(cum_ready, f + 1)
                            gate(f, 1)
                    if first:
                        for q, slot in enumerate(LOGIT_SLOT):
                            if u == slot:
                                if q == 0:
                                    pe.wait_ge(vp_ready, 1)
                                if q == 2:
                                    pe.wait_ge(rest_ready, 4 + 2)
                                routing_logits(q)
                            if u == slot + 1:
                                transpose_logits(q)
                        if u in PAIR_SLOT:
                            if PAIR_SLOT.index(u) == X_GROUPS[2][0]:
                                pe.wait_ge(rest_ready, 4 + 1)
                            transpose_pair(PAIR_SLOT.index(u))
                    if u == (FIRST_V_SLOT if first else V_SLOT) and attend:
                        if not first:
                            pe.wait_ge(silu_ready, f * TILES + 1)
                        pe.wait_ge(xv_ready, i + 1)
                        for c in range(NC):
                            last = nc.tensor.matmul(B_V[:, c * P:(c + 1) * P], xv[:, c * P:(c + 1) * P], wv_s[:],
                                                    start=True, stop=True)
                        last.then_inc(v_ps, 1)
                    if experts:
                        if u == 5:
                            pe.wait_ge(hid_ready, f * TILES + 1)
                            up(f, 1)
                            pe.wait_ge(silu_ready, f * TILES + 2)
                            gate(f, 2)
                        if u == 6:
                            if attend:
                                pe.wait_ge(vp_ready, i + 1)
                            else:
                                pe.wait_ge(silu_ready, f * TILES + 1)
                            up(f, 2)
                        if u == 7:
                            pe.wait_ge(hid_ready, f * TILES + 2)
                            gate(f, 3)
                        if u == 8:
                            pe.wait_ge(silu_ready, f * TILES + 3)
                            up(f, 3)
                        if u == 9:
                            pe.wait_ge(hid_ready, f * TILES + 3)
                            gate(f, 4)
                        if u == 10:
                            pe.wait_ge(silu_ready, f * TILES + 4)
                            up(f, 4)
                    if project and u in project_slots:
                        t = project_slots.index(u)
                        if t == 1 and second:
                            pe.wait_ge(per_e_ready, HALVES)
                            pe.wait_ge(hid_ready, TILES)
                            for h in range(HALVES):
                                last = nc.tensor.matmul(B_Q1[:, 0:2 * E], ones[:, 0:P],
                                                        per_e[:, h].rearrange("p a e -> p (a e)"),
                                                        start=(h == 0), stop=(h == HALVES - 1))
                            last.then_inc(wmean_ps, 1)
                        if t == 0:
                            pe.wait_ge(xb_ready, n + 1)
                            if experts:
                                pe.wait_ge(hid_ready, f * TILES + 4)
                            else:
                                pe.wait_ge(xnT_ready, 2 * X_GROUPS[1][1])
                        if t == 1:
                            if experts:
                                pe.wait_ge(silu_ready, f * TILES + 5)
                            else:
                                pe.wait_ge(logits_ready, 2)
                        if t == 2:
                            if experts:
                                pe.wait_ge(hid_ready, f * TILES + 5)
                                if second:
                                    pe.wait_ge(wmean_copied, 1)
                            else:
                                pe.wait_ge(xnT_ready, NB)
                        if t == 3:
                            pe.wait_ge(rest_ready, n * 4 + 1)
                        project_tile(n, t)
                    if final and u == 11:
                        pe.wait_ge(silu_ready, f * TILES + TILES)
                        for t in range(TILES):
                            pe.wait_ge(hid_ready, f * TILES + t + 1)
                            if t < TILES - 1:
                                pe.wait_ge(hid_masked, f * (TILES - 1) + t + 1)
                            for c in range(NC):
                                down(f, c, t)
                    elif experts and not final and DOWN_SLOT <= u < DOWN_SLOT + NC:
                        if u == DOWN_SLOT:
                            if project:
                                pe.wait_ge(rest_ready, n * 4 + 2)
                            if second:
                                pe.wait_ge(wd_ready, E)
                            pe.wait_ge(hid_ready, f * TILES + TILES)
                            pe.wait_ge(hid_masked, f * (TILES - 1) + TILES - 1)
                        for t in range(TILES):
                            down(f, u - DOWN_SLOT, t)
                    if experts and u == SLOTS - 1:
                        attention_out(f)
                    if j > 0:
                        if g == 0 and experts and not final:
                            weighted(f, NG - 1, j - 1)
                        elif g > 0 and attend:
                            weighted(i, g - 1, j - 1)
                    if second and u == SEL_SLOT:
                        pe.wait_ge(sel_ready, HALVES)
                        pe.wait_ge(rest_ready, i * 4 + 3)
                        for q in range(QUADS):
                            last = nc.tensor.transpose(
                                ps_x[0][:, q * P:(q + 1) * P],
                                sel[:, 4 * q:4 * q + 4].rearrange("p b e c -> p (b e c)"), ident[:])
                        last.then_inc(selT_ps, 1)

            transpose_pair(0)
            pe.wait_ge(wp_split, 1)
            pe.wait_ge(xb_ready, 1)
            for t in range(4):
                project_tile(0, t)
            pe.wait_ge(rest_ready, 4)
            iteration(0, True, False, True)
            iteration(1, True, True, True)
            with pe.Fori(2, NB - 1) as i:
                iteration(i, True, True, True)
            iteration(NB - 1, True, True, False)
            iteration(NB, False, True, False)


def _layouts(v):
    import numpy as np
    a = {k: np.asarray(x) for k, x in v.items()}
    gate = np.concatenate([a['L0_ffn_expert_gate_w'].reshape(E * I, D), a['L0_ffn_shared_gate_w']]).T
    up = np.concatenate([a['L0_ffn_expert_up_w'].reshape(E * I, D), a['L0_ffn_shared_up_w']]).T
    qk = [a[n].reshape(D, NOCT, OCT, F).transpose(0, 1, 3, 2).reshape(D, H * F) for n in ('L0_attn_Wq', 'L0_attn_Wk')]
    wv = a['L0_attn_Wv'].reshape(D, NG, GROUP, DV).transpose(0, 2, 1, 3).reshape(D, H * DV)
    wo = a['L0_attn_Wo'].reshape(NG, GROUP, DV, D).transpose(1, 0, 2, 3).reshape(H * DV, D)
    down = np.concatenate([a['L0_ffn_expert_down_w'].transpose(0, 2, 1).reshape(E * I, D), a['L0_ffn_shared_down_w'].T])
    return {
        'x': a['L0_attn_hidden_states'],
        'w_in': np.concatenate([*qk, wv, gate, up], axis=1),
        'w_v': a['L0_attn_Wv'],
        'w_o': wo,
        'w_down': down.reshape(TILES, P, D).transpose(1, 0, 2),
        'w_route': a['L0_ffn_gate_w'].T,
        'route_bias': a['L0_ffn_lb_bias'],
    }


def kernel(**inputs):
    import numpy as _np
    import concourse.bacc as _bacc
    from concourse import mybir as _mybir
    from concourse.bass_utils import run_bass_kernel_spmd as _run

    nc = _bacc.Bacc("TRN2", target_bir_lowering=False, num_devices=1)
    arrays, args = {}, []
    for name, a in _layouts(inputs).items():
        a = _np.ascontiguousarray(a)
        arrays[f"in_{name}"] = a
        args.append(nc.dram_tensor(f"in_{name}", a.shape, _mybir.dt.from_np(a.dtype), kind="ExternalInput").ap())
    out = nc.dram_tensor("out", (NB, S, D), _mybir.dt.float32, kind="ExternalOutput").ap()
    moe_attention_program(nc, *args, out)
    r = _run(nc, [arrays], core_ids=[0])
    return r.results[0]["out"]
```
